# Optimizing a Trainium2 kernel written in Bass

```python
import numpy as np
import jax
import jax.numpy as jnp

def _softmax(x, axis=-1):
    return jax.nn.softmax(x, axis=axis)

def _gelu(x):
    return jax.nn.gelu(x, approximate=True)

def _silu(x):
    return jax.nn.silu(x)

def _sigmoid(x):
    return jax.nn.sigmoid(x)

def _layernorm(x, axis=-1, eps=1e-05):
    m = jnp.mean(x, axis=axis, keepdims=True)
    v = jnp.var(x, axis=axis, keepdims=True)
    return (x - m) / jnp.sqrt(v + eps)

def _scatter_add(tgt, idx, src, axis=0):
    return tgt.at[idx].add(src)

def _segment_sum(src, seg, n):
    return jax.ops.segment_sum(src, seg, n)
kernel_name = 'mk_gnn_ffn_d1_gnn_r8_fc8409'

def setup_inputs(seed: int=0):
    np.random.seed(seed)
    _w = jnp.asarray

    def _rec_inputs():
        import jax
        import jax.numpy as jnp
        _gk = jax.random.key(seed)
        x = -8.776e-05 + 1 * jax.random.normal(jax.random.fold_in(_gk, 1), (6250, 256), jnp.float32)
        _s = jax.random.randint(jax.random.fold_in(_gk, 2), (100000,), 0, 6250, jnp.int32)
        _d = jax.random.randint(jax.random.fold_in(_gk, 3), (100000,), 0, 6250, jnp.int32)
        _loop = jnp.arange(6250, dtype=jnp.int32)
        src = jnp.concatenate([_s, _d, _loop])
        dst = jnp.concatenate([_d, _s, _loop])
        _o = jnp.argsort(dst, stable=True)
        src = src[_o]
        dst = dst[_o]
        return (x, src, dst)
    x, src, dst = _rec_inputs()

    def _L0_gnn_setup():
        import jax, jax.numpy as jnp
        import numpy as np
        H, D = (8, 32)
        LN_EPS = 1e-05

        def _layernorm(x, g, b):
            mu = jnp.mean(x, axis=-1, keepdims=True)
            var = jnp.mean((x - mu) ** 2, axis=-1, keepdims=True)
            return (x - mu) * jax.lax.rsqrt(var + LN_EPS) * g + b
        key = jax.random.key(seed)
        ks = jax.random.split(key, 8)
        N, E, F = (2500, 40000, 256)
        s = 1.0 / np.sqrt(F)
        return {'feat': jax.random.normal(ks[0], (N, F), jnp.float32), 'edge_src': jax.random.randint(ks[1], (E,), 0, N), 'edge_dst': jax.random.randint(ks[2], (E,), 0, N), 'Wq': jax.random.normal(ks[3], (F, H * D), jnp.float32) * s, 'Wk': jax.random.normal(ks[4], (F, H * D), jnp.float32) * s, 'Wv': jax.random.normal(ks[5], (F, H * D), jnp.float32) * s, 'ln_g': jnp.ones((F,), jnp.float32), 'ln_b': jnp.zeros((F,), jnp.float32), 'W1': jax.random.normal(ks[6], (F, 4 * F), jnp.float32) * s, 'b1': jnp.zeros((4 * F,), jnp.float32), 'prelu_alpha': jnp.full((4 * F,), 0.25, jnp.float32), 'W2': jax.random.normal(ks[7], (4 * F, F), jnp.float32) * (1.0 / np.sqrt(4 * F)), 'b2': jnp.zeros((F,), jnp.float32)}
    _L0_gnn_all = _L0_gnn_setup()
    _L0_gnn_in = {k: v for k, v in _L0_gnn_all.items() if k in ('Wq', 'Wk', 'Wv', 'ln_g', 'ln_b', 'W1', 'b1', 'prelu_alpha', 'W2', 'b2')}
    del _L0_gnn_all

    def _L0_ffn_setup():
        import jax, jax.numpy as jnp
        import numpy as np
        NUM_EXPERTS = 8
        TOP_K = 2
        B, S, D = (8, 1024, 256)

        def _moe(tokens, router_w, w1, b1, w2, b2):
            N = tokens.shape[0]
            E = router_w.shape[0]
            logits = tokens.astype(jnp.float32) @ router_w.astype(jnp.float32).T
            probs = jax.nn.softmax(logits, axis=-1)
            rw, re = jax.lax.top_k(probs, TOP_K)
            if TOP_K > 1:
                rw = rw / jnp.maximum(rw.sum(-1, keepdims=True), 1e-12)
            rw = rw.astype(tokens.dtype)
            combine = jnp.zeros((N, E), tokens.dtype).at[jnp.arange(N)[:, None], re].set(rw)
            out = tokens
            for e in range(E):
                h = jax.nn.gelu(tokens @ w1[e] + b1[e], approximate=False)
                y = h @ w2[e] + b2[e]
                out = out + combine[:, e:e + 1] * y
            return out
        key = jax.random.key(seed)
        ks = jax.random.split(key, 4)
        scale = 1.0 / np.sqrt(D).astype(np.float32)
        return {'input_embeddings': jax.random.normal(ks[0], (B, S, D), jnp.float32), 'router_w': jax.random.normal(ks[1], (NUM_EXPERTS, D), jnp.float32) * scale, 'w1': jax.random.normal(ks[2], (NUM_EXPERTS, D, D), jnp.float32) * scale, 'b1': jnp.zeros((NUM_EXPERTS, D), jnp.float32), 'w2': jax.random.normal(ks[3], (NUM_EXPERTS, D, D), jnp.float32) * scale, 'b2': jnp.zeros((NUM_EXPERTS, D), jnp.float32)}
    _L0_ffn_all = _L0_ffn_setup()
    _L0_ffn_in = {k: v for k, v in _L0_ffn_all.items() if k in ('router_w', 'w1', 'b1', 'w2', 'b2')}
    del _L0_ffn_all
    return {'x': x, 'src': src, 'dst': dst, 'L0_gnn_Wq': _L0_gnn_in['Wq'], 'L0_gnn_Wk': _L0_gnn_in['Wk'], 'L0_gnn_Wv': _L0_gnn_in['Wv'], 'L0_gnn_ln_g': _L0_gnn_in['ln_g'], 'L0_gnn_ln_b': _L0_gnn_in['ln_b'], 'L0_gnn_W1': _L0_gnn_in['W1'], 'L0_gnn_b1': _L0_gnn_in['b1'], 'L0_gnn_prelu_alpha': _L0_gnn_in['prelu_alpha'], 'L0_gnn_W2': _L0_gnn_in['W2'], 'L0_gnn_b2': _L0_gnn_in['b2'], 'L0_ffn_router_w': _L0_ffn_in['router_w'], 'L0_ffn_w1': _L0_ffn_in['w1'], 'L0_ffn_b1': _L0_ffn_in['b1'], 'L0_ffn_w2': _L0_ffn_in['w2'], 'L0_ffn_b2': _L0_ffn_in['b2']}

def reference(x, src, dst, L0_gnn_Wq, L0_gnn_Wk, L0_gnn_Wv, L0_gnn_ln_g, L0_gnn_ln_b, L0_gnn_W1, L0_gnn_b1, L0_gnn_prelu_alpha, L0_gnn_W2, L0_gnn_b2, L0_ffn_router_w, L0_ffn_w1, L0_ffn_b1, L0_ffn_w2, L0_ffn_b2):
    import jax
    import jax.numpy as jnp

    def _L0_gnn_ref(feat, edge_src, edge_dst, Wq, Wk, Wv, ln_g, ln_b, W1, b1, prelu_alpha, W2, b2):
        import jax, jax.numpy as jnp
        import numpy as np
        H, D = (8, 32)
        LN_EPS = 1e-05

        def _layernorm(x, g, b):
            mu = jnp.mean(x, axis=-1, keepdims=True)
            var = jnp.mean((x - mu) ** 2, axis=-1, keepdims=True)
            return (x - mu) * jax.lax.rsqrt(var + LN_EPS) * g + b
        N = feat.shape[0]
        feat_c = jax.lax.stop_gradient(feat)
        q = (feat @ Wq).reshape(N, H, D)
        k = (feat_c @ Wk).reshape(N, H, D)
        v = (feat_c @ Wv).reshape(N, H, D)
        e = jnp.einsum('ehd,ehd->eh', k[edge_src], q[edge_dst]) / np.sqrt(H * D)
        m = jax.ops.segment_max(e, edge_dst, num_segments=N)
        p = jnp.exp(e - m[edge_dst])
        z = jax.ops.segment_sum(p, edge_dst, num_segments=N)
        a = p / z[edge_dst]
        msg = v[edge_src] * a[:, :, None]
        ft2 = jax.ops.segment_sum(msg, edge_dst, num_segments=N)
        rst = ft2.reshape(feat.shape) + feat
        rst = _layernorm(rst, ln_g, ln_b)
        h = rst @ W1 + b1
        h = jnp.where(h > 0, h, prelu_alpha * h)
        ffn = h @ W2 + b2
        rst = _layernorm(rst + ffn, ln_g, ln_b)
        return rst

    def _L0_ffn_ref(input_embeddings, router_w, w1, b1, w2, b2):
        import jax, jax.numpy as jnp
        import numpy as np
        NUM_EXPERTS = 8
        TOP_K = 2
        B, S, D = (8, 1024, 256)

        def _moe(tokens, router_w, w1, b1, w2, b2):
            N = tokens.shape[0]
            E = router_w.shape[0]
            logits = tokens.astype(jnp.float32) @ router_w.astype(jnp.float32).T
            probs = jax.nn.softmax(logits, axis=-1)
            rw, re = jax.lax.top_k(probs, TOP_K)
            if TOP_K > 1:
                rw = rw / jnp.maximum(rw.sum(-1, keepdims=True), 1e-12)
            rw = rw.astype(tokens.dtype)
            combine = jnp.zeros((N, E), tokens.dtype).at[jnp.arange(N)[:, None], re].set(rw)
            out = tokens
            for e in range(E):
                h = jax.nn.gelu(tokens @ w1[e] + b1[e], approximate=False)
                y = h @ w2[e] + b2[e]
                out = out + combine[:, e:e + 1] * y
            return out
        b, s, d = input_embeddings.shape
        tokens = input_embeddings.reshape(b * s, d)
        return _moe(tokens, router_w, w1, b1, w2, b2).reshape(b, s, d)
    x = x + _L0_gnn_ref(_layernorm(x, axis=-1), src, dst, L0_gnn_Wq, L0_gnn_Wk, L0_gnn_Wv, L0_gnn_ln_g, L0_gnn_ln_b, L0_gnn_W1, L0_gnn_b1, L0_gnn_prelu_alpha, L0_gnn_W2, L0_gnn_b2)
    x = x + _L0_ffn_ref(_layernorm(x, axis=-1)[None], L0_ffn_router_w, L0_ffn_w1, L0_ffn_b1, L0_ffn_w2, L0_ffn_b2)[0]
    return x

_drawn_inputs = setup_inputs


def setup_inputs(seed=0):
    import zlib

    import numpy as np

    out = dict(_drawn_inputs(seed))
    spreads = {'L0_gnn_ln_g': (1.0, 0.2),
     'L0_gnn_ln_b': (0.0, 0.1),
     'L0_gnn_b1': (0.0, 0.1),
     'L0_gnn_prelu_alpha': (0.25, 0.6),
     'L0_gnn_b2': (0.0, 0.1),
     'L0_ffn_b1': (0.0, 0.471),
     'L0_ffn_b2': (0.0, 0.321)}
    factors = {}
    for name, (base, spread) in spreads.items():
        noise = np.random.default_rng([zlib.crc32(name.encode()), seed]).standard_normal(out[name].shape)
        drawn = base * np.exp(spread * noise) if base else spread * noise
        out[name] = jnp.asarray(drawn.astype(out[name].dtype))
    for name, factor in factors.items():
        out[name] = (out[name] * factor).astype(out[name].dtype)
    return out
```

```python
from contextlib import ExitStack

import concourse.bass as bass
from concourse import mybir

ALU = mybir.AluOpType
ACT = mybir.ActivationFunctionType
AX = mybir.AxisListType
F32 = mybir.dt.float32
BF16 = mybir.dt.bfloat16
I32 = mybir.dt.int32

P = 128
SUB = 4
ITEM = P * SUB
RING = 6
HEADS = 8
DH = 32
F = HEADS * DH
HC = DH + 1
FA = HEADS * HC
BIG = 2.0 ** 125
STEPS = 77
EPS = 1e-5


class Sizes:

    def __init__(self, nodes, edges, hidden, experts):
        self.N, self.E, self.H1, self.X = nodes, edges, hidden, experts
        self.NT = -(-nodes // P)
        self.TB = max(b for b in range(1, 8) if self.NT % b == 0)
        self.NB = self.NT // self.TB
        self.tail = nodes - (self.NT - 1) * P
        items = edges // ITEM + self.NT
        self.NI = -(-items // RING) * RING
        self.L = -(-(edges + ITEM) // P)
        self.EP = P * self.L
        self.PAD = self.NT * P + 1024
        assert self.NI <= 512 and self.NT + 1 <= P and nodes % P


def affine_identity(nc, pool, tile, size, zeroed, done):
    nc.gpsimd.memset(tile, 0.0).then_inc(zeroed, 1)
    pool.wait_ge(zeroed, 1)
    nc.gpsimd.affine_select(out=tile, in_=tile, compare_op=ALU.not_equal, fill=1.0, base=0,
                            pattern=[[-1, size]], channel_multiplier=1).then_inc(done, 1)


def rsqrt(nc, step, var, rstd, tmp):
    step(nc.vector.tensor_scalar(tmp.bitcast(I32), var.bitcast(I32), 1, None, ALU.logical_shift_right))
    step(nc.vector.tensor_scalar(rstd.bitcast(I32), tmp.bitcast(I32), -1.0, float(0x5F3759DF), ALU.mult, ALU.add))
    for _ in range(3):
        step(nc.vector.tensor_tensor(tmp, rstd, rstd, ALU.mult))
        step(nc.vector.scalar_tensor_tensor(out=tmp, in0=tmp, scalar=-0.5, in1=var, op0=ALU.mult, op1=ALU.mult))
        step(nc.vector.scalar_tensor_tensor(out=rstd, in0=tmp, scalar=1.5, in1=rstd, op0=ALU.add, op1=ALU.mult))


class Chain:

    def __init__(self, eng, sem):
        self.eng, self.sem, self.k, self.base = eng, sem, 0, 0

    def __call__(self, ins, apart=None):
        ins.then_inc(self.sem, 1)
        self.k += 1
        self.eng.wait_ge(self.sem, self.base + self.k)
        if apart is not None:
            self.eng.sem_inc(apart, 1)


def node_phase(nc, z, x, src, dst, Wq, Wk, Wv, feat_d, kv_d, etab_d, pen_d, keep):
    TB, NB, L = z.TB, z.NB, z.L
    with ExitStack() as ctx:
        def sb(name, shape, dt=F32):
            return ctx.enter_context(nc.sbuf_tensor("n_" + name, shape, dt))

        def sem(name):
            return ctx.enter_context(nc.semaphore("n_" + name))

        w_sb = sb("w_qkv", [P, 2, 3 * F])
        x_sb = sb("x_in", [P, TB, F])
        feat = sb("feat", [P, TB, F])
        featT = sb("featT", [P, 2, 2, P])
        kv_out = sb("kv_out", [P, TB, 2 * F])
        stats = sb("stats", [P, TB, 6])
        mv = sb("mv", [P, TB, 2])
        var = sb("var", [P, TB])
        rstd = sb("rstd", [P, TB])
        tmp = sb("tmp", [P, TB])
        idx_i = sb("idx_i", [P, L], I32)
        src_f = sb("src_f", [P, L])
        dst_f = sb("dst_f", [P, L])
        nxt_f = sb("nxt_f", [P, L])
        junk = sb("junk", [P, L], BF16)
        below = sb("below", [P, z.NT + 1])
        thr = sb("thr", [P, z.E // ITEM + 2])
        junk2 = sb("junk2", [P, z.E // ITEM + 2])
        item_no = sb("item_no", [P, z.NI])
        tri = sb("tri", [P, P])
        seg = sb("seg", [P, 4])
        spread = sb("spread", [P, 2, P])
        mask = sb("mask", [P, z.NI])
        tabf = sb("tabf", [P, 2, z.NI])

        ps_xT = [ctx.enter_context(nc.psum_tensor(f"ps_xT{i}", [P, 512], F32)) for i in range(2)]
        ps_kv = [ctx.enter_context(nc.psum_tensor(f"ps_kv{i}", [P, 512], F32)) for i in range(2)]
        ps_q = [ctx.enter_context(nc.psum_tensor(f"ps_q{i}", [P, 512], F32)) for i in range(2)]
        ps_n = ctx.enter_context(nc.psum_tensor("ps_n", [P, 512], F32))
        ps_m = ctx.enter_context(nc.psum_tensor("ps_m", [P, 512], F32))

        w_in = sem("w_in")
        x_in = sem("x_loaded")
        x_init = sem("x_init")
        feat_out = sem("feat_stored")
        kv_stored = sem("kv_stored")
        feat_rdy = sem("feat_ready")
        xT_ps = sem("xT_in_psum")
        xT_rdy = sem("xT_ready")
        kv_ps = sem("kv_in_psum")
        q_ps = sem("q_in_psum")
        kv_rdy = sem("kv_evacuated")
        q_rdy = sem("q_evacuated")
        dvec = sem("dve_step")
        passed = sem("dve_passed")
        idz = sem("ident_zeroed")
        iddone = sem("ident_done")
        cst = sem("pool_constants")
        trid = sem("tri_set")
        dst_in = sem("dst_loaded")
        src_in = sem("src_loaded")
        nxt_in = sem("next_loaded")
        padded = sem("index_tile_padded")
        tabs = sem("edge_tables_ready")
        tab_out = sem("edge_tables_stored")
        cnt_rdy = sem("counts_ready")
        seg_ps = sem("segments_in_psum")
        item_rdy = sem("items_ready")
        base_ps = sem("bases_in_psum")
        mask_rdy = sem("mask_ready")
        w_ps = sem("w_in_psum")
        w_got = sem("w_read")
        sb_ps = sem("starts_in_psum")

        full = z.E // L
        rest = z.E - full * L
        full1 = (z.E - 1) // L
        rest1 = z.E - 1 - full1 * L
        xb = x[0:(z.NT - 1) * P, :].rearrange("(t p) f -> p t f", p=P)
        featb = feat_d.rearrange("(t p) f -> p t f", p=P)
        kvb = kv_d.rearrange("(t p) f -> t p f", p=P)
        block = ctx.enter_context(nc.Block())

        @block.sync
        def _(sp):
            for i, w in enumerate((Wk, Wv, Wq)):
                sp.dma_start(w_sb[:, :, i * F:(i + 1) * F], w.rearrange("(c p) n -> p c n", p=P)).then_inc(w_in, 16)
            sp.wait_ge(x_init, 1)
            if NB > 1:
                with sp.Fori(0, NB - 1) as b:
                    sp.wait_ge(feat_rdy, b * TB)
                    sp.dma_start(x_sb[:, :, :], xb[:, bass.ds(b * TB, TB), :]).then_inc(x_in, 32)
            sp.wait_ge(feat_rdy, (NB - 1) * TB)
            if TB > 1:
                sp.dma_start(x_sb[:, 0:TB - 1, :], xb[:, (NB - 1) * TB:NB * TB - 1, :]).then_inc(x_in, 16)
            sp.dma_start(x_sb[0:z.tail, TB - 1, :], x[(z.NT - 1) * P:z.N, :]).then_inc(x_in, 16)
            sp.wait_ge(tabs, 1)
            for i, t in enumerate((src_f, dst_f, nxt_f)):
                sp.dma_start(etab_d[i].rearrange("(p l) -> p l", p=P), t[:, :]).then_inc(tab_out, 16)
            sp.wait_ge(tabs, 2)
            sp.dma_start(pen_d[1:1 + z.EP].rearrange("(p l) -> p l", p=P), dst_f[:, :]).then_inc(tab_out, 16)
            sp.dma_start(pen_d[0:1].rearrange("(a b) -> a b", a=1), below[0:1, 0:1]).then_inc(tab_out, 16)
            sp.wait_ge(tab_out, 16 * 5)
            sp.wait_ge(feat_out, 16 * NB)
            sp.wait_ge(kv_stored, 16 * z.NT)

        @block.gpsimd
        def _(pool):
            affine_identity(nc, pool, keep.ident[:, :], P, idz, iddone)
            nc.gpsimd.iota(keep.iota[:, :], [[1, P]], base=0, channel_multiplier=0,
                           allow_small_or_imprecise_dtypes=True).then_inc(cst, 1)
            nc.gpsimd.iota(keep.iota8[:, :], [[-1, HEADS]], base=HEADS, channel_multiplier=0,
                           allow_small_or_imprecise_dtypes=True).then_inc(cst, 1)
            nc.gpsimd.iota(thr[:, :], [[ITEM, z.E // ITEM + 2]], base=0, channel_multiplier=0,
                           allow_small_or_imprecise_dtypes=True).then_inc(cst, 1)
            nc.gpsimd.iota(item_no[:, :], [[1, z.NI]], base=0, channel_multiplier=0,
                           allow_small_or_imprecise_dtypes=True).then_inc(cst, 1)
            nc.gpsimd.memset(tri[:, :], 1.0).then_inc(trid, 1)
            pool.wait_ge(trid, 1)
            nc.gpsimd.affine_select(out=tri[:, :], in_=tri[:, :], compare_op=ALU.is_ge, fill=0.0, base=0,
                                    pattern=[[1, P]], channel_multiplier=-1).then_inc(trid, 1)
            nc.gpsimd.memset(keep.acc[:, :], 0.0).then_inc(cst, 1)
            nc.gpsimd.memset(idx_i[:, :], z.PAD).then_inc(padded, 1)
            pool.wait_ge(padded, 1)
            pool.dma_start(idx_i[0:full, :], dst[0:full * L].rearrange("(p l) -> p l", l=L)).then_inc(dst_in, 16)
            pool.dma_start(idx_i[full:full + 1, 0:rest], dst[full * L:z.E].rearrange("(a l) -> a l", a=1)).then_inc(dst_in, 16)
            pool.wait_ge(cnt_rdy, 1)
            nc.gpsimd.memset(idx_i[:, :], z.PAD).then_inc(padded, 1)
            pool.wait_ge(padded, 2)
            pool.dma_start(idx_i[0:full1, :], dst[1:1 + full1 * L].rearrange("(p l) -> p l", l=L)).then_inc(nxt_in, 16)
            pool.dma_start(idx_i[full1:full1 + 1, 0:rest1],
                           dst[1 + full1 * L:z.E].rearrange("(a l) -> a l", a=1)).then_inc(nxt_in, 16)
            pool.wait_ge(cnt_rdy, 2)
            nc.gpsimd.memset(idx_i[:, :], 0).then_inc(padded, 1)
            pool.wait_ge(padded, 3)
            pool.dma_start(idx_i[0:full, :], src[0:full * L].rearrange("(p l) -> p l", l=L)).then_inc(src_in, 16)
            pool.dma_start(idx_i[full:full + 1, 0:rest], src[full * L:z.E].rearrange("(a l) -> a l", a=1)).then_inc(src_in, 16)

        @block.scalar
        def _(act):
            with act.Fori(0, NB) as b:
                act.wait_ge(feat_rdy, (b + 1) * TB)
                act.dma_start(featb[:, bass.ds(b * TB, TB), :], feat[:, :, :]).then_inc(feat_out, 16)
                for j in range(TB):
                    t = b * TB + j
                    act.wait_ge(kv_ps, t + 1)
                    if j == 0:
                        act.wait_ge(kv_stored, 16 * TB * b)
                    nc.scalar.activation(kv_out[:, j, :], ps_kv[j % 2][:, :], ACT.Copy).then_inc(kv_rdy, 1)
                    act.wait_ge(q_ps, t + 1)
                    nc.scalar.activation(keep.q[:, bass.ds(t * F, F)], ps_q[j % 2][:, 0:F], ACT.Copy,
                                         scale=float(F) ** -0.5).then_inc(q_rdy, 1)
                    act.wait_ge(kv_rdy, t + 1)
                    act.dma_start(kvb[bass.ds(t, 1), :, :].rearrange("a p f -> (a p) f"), kv_out[:, j, :]).then_inc(kv_stored, 16)

        @block.tensor
        def _(pe):
            pe.wait_ge(w_in, 48)
            pe.wait_ge(iddone, 1)
            with pe.Fori(0, NB) as b:
                for j in range(TB):
                    t = b * TB + j
                    s = j % 2
                    pe.wait_ge(feat_rdy, t + 1)
                    if j == 0:
                        pe.wait_ge(xT_rdy, t)
                    elif j >= 2:
                        pe.wait_ge(xT_rdy, t - 1)
                    for c in range(2):
                        mm = nc.tensor.transpose(ps_xT[s][:, c * P:(c + 1) * P], feat[:, j, c * P:(c + 1) * P],
                                                 keep.ident[:, :])
                    mm.then_inc(xT_ps, 1)
                    pe.wait_ge(xT_rdy, t + 1)
                    if j == 0:
                        pe.wait_ge(kv_rdy, t)
                        pe.wait_ge(q_rdy, t)
                    elif j >= 2:
                        pe.wait_ge(kv_rdy, t - 1)
                        pe.wait_ge(q_rdy, t - 1)
                    for c in range(2):
                        mm = nc.tensor.matmul(ps_kv[s][:, :], featT[:, s, c, :], w_sb[:, c, 0:2 * F],
                                              start=(c == 0), stop=(c == 1))
                    mm.then_inc(kv_ps, 1)
                    for c in range(2):
                        mm = nc.tensor.matmul(ps_q[s][:, 0:F], featT[:, s, c, :], w_sb[:, c, 2 * F:3 * F],
                                              start=(c == 0), stop=(c == 1))
                    mm.then_inc(q_ps, 1)
            pe.wait_ge(cnt_rdy, 2)
            nc.tensor.matmul(ps_n[0:z.NT, 0:1], below[:, 0:z.NT], keep.ones[:, 0:1], start=True, stop=True)
            nc.tensor.matmul(ps_n[0:z.NT, 1:2], below[:, 1:z.NT + 1], keep.ones[:, 0:1], start=True,
                             stop=True).then_inc(seg_ps, 1)
            pe.wait_ge(item_rdy, 1)
            pe.wait_ge(trid, 2)
            nc.tensor.matmul(ps_n[0:z.NT, 2:3], tri[0:z.NT, 0:z.NT], seg[0:z.NT, 3:4], start=True,
                             stop=True).then_inc(base_ps, 1)
            pe.wait_ge(mask_rdy, 1)
            nc.tensor.matmul(ps_m[:, 0:z.NI], keep.ones[0:z.NT, :], mask[0:z.NT, :], start=True, stop=True).then_inc(w_ps, 1)
            nc.tensor.matmul(ps_n[:, 0:z.NI], spread[0:z.NT, 0, :], mask[0:z.NT, :], start=True, stop=True).then_inc(sb_ps, 1)
            pe.wait_ge(w_got, 1)
            nc.tensor.matmul(ps_m[:, 0:z.NI], spread[0:z.NT, 1, :], mask[0:z.NT, :], start=True, stop=True).then_inc(sb_ps, 1)

        @block.vector
        def _(dve):
            step = Chain(dve, dvec)
            nc.vector.memset(x_sb[:, :, :], 0.0).then_inc(x_init, 1)
            step(nc.vector.memset(keep.ones[:, :], 1.0))
            pre = step.k
            with dve.Fori(0, NB) as b:
                per = 14
                step.k, step.base = 0, pre + b * per
                dve.wait_ge(x_in, 32 * (b + 1))
                for j in range(TB):
                    last = nc.vector.bn_stats(stats[:, j, :], x_sb[:, j, :])
                step(last, apart=passed)
                for j in range(TB):
                    last = nc.vector.bn_aggr(mv[:, j, :], stats[:, j, :])
                step(last)
                step(nc.vector.tensor_scalar(var[:, :], mv[:, :, 1], EPS, None, ALU.add))
                rsqrt(nc, step, var[:, :], rstd[:, :], tmp[:, :])
                assert step.k == per
                dve.wait_ge(feat_out, 16 * b)
                for j in range(TB):
                    t = b * TB + j
                    if j == 0:
                        dve.wait_ge(xT_ps, t)
                    nc.vector.tensor_scalar(feat[:, j, :], x_sb[:, j, :], mv[:, j, 0:1], rstd[:, j:j + 1],
                                            ALU.subtract, ALU.mult).then_inc(feat_rdy, 1)
                for j in range(TB):
                    t = b * TB + j
                    dve.wait_ge(xT_ps, t + 1)
                    if j == 0:
                        dve.wait_ge(q_ps, t)
                    elif j >= 2:
                        dve.wait_ge(q_ps, t - 1)
                    nc.vector.tensor_copy(featT[:, j % 2, :, :],
                                          ps_xT[j % 2][:, 0:2 * P].rearrange("p (c n) -> p c n", c=2)).then_inc(xT_rdy, 1)
            step.k, step.base = 0, pre + NB * per
            dve.wait_ge(dst_in, 32)
            nc.vector.tensor_copy(dst_f[:, :], idx_i[:, :]).then_inc(cnt_rdy, 1)
            dve.wait_ge(cnt_rdy, 1)
            step(nc.vector.memset(below[:, :], 0.0))
            for w in range(1, z.NT + 1):
                step(nc.vector.tensor_scalar(junk[:, :], dst_f[:, :], float(P * w), 0.0, ALU.is_lt, ALU.add,
                                             accum_out=below[:, w:w + 1]))
            dve.wait_ge(nxt_in, 32)
            nc.vector.tensor_copy(nxt_f[:, :], idx_i[:, :]).then_inc(cnt_rdy, 1)
            dve.wait_ge(cnt_rdy, 2)
            step(nc.vector.tensor_tensor(nxt_f[:, :], nxt_f[:, :], dst_f[:, :], ALU.not_equal))
            step(nc.vector.tensor_scalar(nxt_f[:, :], nxt_f[:, :], BIG, None, ALU.mult))
            dve.wait_ge(src_in, 32)
            nc.vector.tensor_copy(src_f[:, :], idx_i[:, :]).then_inc(tabs, 1)
            dve.wait_ge(tab_out, 48)
            nc.vector.tensor_scalar(dst_f[:, :], nxt_f[:, :], -1.0, None, ALU.mult).then_inc(tabs, 1)
            dve.wait_ge(iddone, 1)
            step(nc.vector.tensor_copy(keep.identb[:, :], keep.ident[:, :]))
            nt = z.NT
            dve.wait_ge(seg_ps, 1)
            step(nc.vector.tensor_copy(seg[0:nt, 0:2], ps_n[0:nt, 0:2]))
            step(nc.vector.tensor_tensor(seg[0:nt, 2:3], seg[0:nt, 1:2], seg[0:nt, 0:1], ALU.subtract))
            dve.wait_ge(cst, 4)
            nc.vector.tensor_scalar(junk2[0:nt, :], thr[0:nt, :], seg[0:nt, 2:3], 0.0, ALU.is_lt, ALU.add,
                                    accum_out=seg[0:nt, 3:4]).then_inc(item_rdy, 1)
            dve.wait_ge(item_rdy, 1)
            for i in range(2):
                step(nc.vector.tensor_scalar(spread[0:nt, i, :], keep.ones[0:nt, :], seg[0:nt, 2 + i:3 + i], None, ALU.mult))
            dve.wait_ge(base_ps, 1)
            nc.vector.tensor_scalar(mask[0:nt, :], item_no[0:nt, :], ps_n[0:nt, 2:3], None, ALU.is_ge).then_inc(mask_rdy, 1)
            dve.wait_ge(w_ps, 1)
            nc.vector.tensor_scalar(tabf[:, 0, :], ps_m[:, 0:z.NI], float(nt - 1), None, ALU.min).then_inc(w_got, 1)
            dve.wait_ge(w_got, 1)
            step(nc.vector.tensor_copy(keep.w_i[:, :], tabf[:, 0, :]))
            step(nc.vector.tensor_scalar(keep.minus_first[:, :], tabf[:, 0, :], -float(P), None, ALU.mult))
            dve.wait_ge(sb_ps, 2)
            step(nc.vector.tensor_tensor(tabf[:, 1, :], item_no[:, :], ps_m[:, 0:z.NI], ALU.subtract))
            step(nc.vector.scalar_tensor_tensor(out=tabf[:, 1, :], in0=tabf[:, 1, :], scalar=float(ITEM),
                                                in1=ps_n[:, 0:z.NI], op0=ALU.mult, op1=ALU.add))
            step(nc.vector.tensor_scalar(keep.e_i[:, :], tabf[:, 1, :], float(z.E), None, ALU.min))
            step(nc.vector.tensor_tensor(tabf[:, 0, 1:z.NI], keep.minus_first[:, 1:z.NI], keep.minus_first[:, 0:z.NI - 1], ALU.not_equal))
            step(nc.vector.memset(keep.reset[:, 0:1], -2.0 * BIG))
            step(nc.vector.tensor_scalar(keep.reset[:, 1:z.NI], tabf[:, 0, 1:z.NI], -2.0 * BIG, None, ALU.mult))
            step(nc.vector.tensor_scalar(keep.lastcol[:, :], keep.ident[:, P - 1:P], BIG, None, ALU.mult))
            step(nc.vector.tensor_scalar(keep.notlast[:, :], keep.ident[:, P - 1:P], -1.0, 1.0, ALU.mult, ALU.add))
            dve.wait_ge(cst, 5)


def edge_phase(nc, z, kv_d, etab_d, pen_d, keep):
    NI, R = z.NI, RING
    with ExitStack() as ctx:
        def sb(name, shape, dt=F32):
            return ctx.enter_context(nc.sbuf_tensor(name, shape, dt))

        def sem(name):
            return ctx.enter_context(nc.semaphore(name))

        rows = sb("idx_rows", [3 * SUB, R, P])
        pen = sb("pen", [SUB * HEADS, R, P])
        idx = sb("idx", [P, R, SUB], I32)
        rel = sb("rel", [P, R, SUB])
        sel = sb("sel", [P, R, SUB, HEADS + 1])
        kv = sb("kv", [P, R, SUB, 2 * F])
        oh16 = sb("oh16", [P, 2, SUB, P], BF16)
        sq = sb("sq", [P, SUB, P], BF16)
        oh32 = sb("oh32", [P, R, SUB, P])
        ohT = sb("ohT", [P, R, SUB, P])
        prod = sb("prod", [P, SUB, F])
        score = sb("score", [P, R, SUB * HEADS])
        run = sb("run", [SUB * HEADS, R, P])
        absent = sb("absent", [P, SUB])
        cand = sb("cand", [P, SUB, HEADS])
        top = sb("top", [P, HEADS])
        mnew = sb("mnew", [P, R, HEADS])
        mdif = sb("mdif", [P, R, HEADS])
        alpha = sb("alpha", [P, R, HEADS])
        arg = sb("arg", [P, R, SUB * HEADS])
        pv = sb("pv", [P, 2, SUB, FA])

        def bank(name, dt=F32):
            return ctx.enter_context(nc.psum_tensor(name, [P, 2048 // (4 if dt == F32 else 2)], dt))

        ps_q = ctx.enter_context(nc.psum_tensor("ps_qx", [P, SUB * F], F32))
        ps_oh = bank("ps_oh", BF16)
        ps_agg = [bank("ps_agg0"), bank("ps_agg1")]
        ps_idx = bank("ps_idx")
        ps_s = bank("ps_scores")
        ps_m = bank("ps_maxima")

        rows_in = [sem(f"rows_loaded{i}") for i in range(R)]
        kv_in = [sem(f"kv_loaded{i}") for i in range(R)]
        idx_ps = sem("idx_in_psum")
        idx_rdy = sem("idx_ready")
        rel_rdy = sem("rel_ready")
        oh_rdy = sem("onehot_ready")
        sq_rdy = sem("squares_ready")
        ohT_ps = sem("onehotT_in_psum")
        ohT_rdy = sem("onehotT_ready")
        oh32_rdy = sem("onehot32_ready")
        q_ps = sem("q_rows_in_psum")
        prod_rdy = sem("prod_ready")
        dots_rdy = sem("dots_ready")
        eT_ps = sem("scoresT_in_psum")
        run_rdy = sem("running_max_ready")
        back_ps = sem("running_max_in_psum")
        sel_rdy = sem("last_selected")
        msel_ps = sem("tile_max_in_psum")
        m_step = sem("max_step")
        first_max = sem("first_max_set")
        m_rdy = sem("new_max_ready")
        me_ps = sem("edge_max_in_psum")
        arg_rdy = sem("exponent_ready")
        p_rdy = sem("p_ready")
        al_rdy = sem("alpha_ready")
        pv_rdy = sem("pv_ready")
        agg_ps = sem("sums_in_psum")
        acc_half = sem("acc_scaled")
        acc_rdy = sem("acc_ready")
        pe_passed = sem("pe_passed")
        pool_passed = sem("pool_passed")

        block = ctx.enter_context(nc.Block())

        def pipeline(eng, step):
            for base in (-R, 0):
                for k in range(R):
                    step(base, k)
            if NI > 2 * R:
                with eng.Fori(1, NI // R - 1) as turn:
                    for k in range(R):
                        step(turn * R, k)
            for base in (NI - R, NI):
                for k in range(R):
                    step(base, k)

        def item(base, k, lag):
            j = k + lag
            if isinstance(base, int):
                n = base + j
                if n < 0 or n >= NI:
                    return None
                return n, j % R
            return base + j, j % R

        def wait(eng, s, value):
            if not (isinstance(value, int) and value <= 0):
                eng.wait_ge(s, value)

        def wait_apart(eng, passed, *waits):
            for sem_, v in waits:
                wait(eng, sem_, v)
            eng.sem_inc(passed, 1)

        def wait_slot(eng, s, n, slot, per):
            if isinstance(n, int):
                eng.wait_ge(s, per * ((n - slot) // R + 1))
            else:
                eng.wait_ge(s, (n - slot + R) // R * per)

        @block.sync
        def _(sp):
            def load(base, k):
                it = item(base, k, 5)
                if it is None:
                    return
                n, s = it
                wait(sp, idx_ps, n - R + 1)
                wait(sp, run_rdy, n - R + 1)
                e = sp.value_load(keep.e_i[0:1, bass.ds(n, 1)], min_val=0, max_val=z.E)
                for i in range(3):
                    sp.dma_start(rows[i * SUB:(i + 1) * SUB, s, :],
                                 etab_d[i, bass.ds(e, ITEM)].rearrange("(g p) -> g p", p=P)).then_inc(rows_in[s], 16)
                for g in range(SUB):
                    sp.dma_start(pen[g * HEADS:(g + 1) * HEADS, s, :],
                                 pen_d[bass.ds(e + g * P, P)].rearrange("(a p) -> a p", a=1).to_broadcast([HEADS, P]),
                                 ).then_inc(rows_in[s], 16)
            pipeline(sp, load)

        LOADS = 16 * (3 + SUB)

        @block.gpsimd
        def _(pool):
            def gather(base, k):
                it = item(base, k, 3)
                if it is None:
                    return
                n, s = it
                wait_apart(pool, pool_passed, (idx_rdy, n + 1), (pv_rdy, n - R + 1))
                for g in range(SUB):
                    pool.indirect_dma_start(
                        out=kv[:, s, g, :], out_offset=None, in_=kv_d,
                        in_offset=bass.IndirectOffsetOnAxis(ap=idx[:, s, g:g + 1], axis=0),
                    ).then_inc(kv_in[s], 16)
            pipeline(pool, gather)

        @block.scalar
        def _(act):
            def go(base, k):
                it = item(base, k, 1)
                if it is not None:
                    n, s = it
                    act.wait_ge(ohT_ps, n + 1)
                    wait(act, me_ps, n - R + 1)
                    nc.scalar.activation(ohT[:, s, :, :], ps_oh[:, 0:SUB * P].rearrange("p (g n) -> p g n", g=SUB),
                                         ACT.Copy).then_inc(ohT_rdy, 1)
                it = item(base, k, -2)
                if it is not None:
                    n, s = it
                    act.wait_ge(arg_rdy, n + 1)
                    wait(act, agg_ps, n - 1)
                    nc.scalar.activation(pv[:, s % 2, :, :].rearrange("p g (h c) -> p (g h) c", c=HC)[:, :, DH],
                                         arg[:, s, :], ACT.Exp).then_inc(p_rdy, 1)
                    wait(act, acc_half, n - 1)
                    nc.scalar.activation(alpha[:, s, :], mdif[:, s, :], ACT.Exp).then_inc(al_rdy, 1)
                it = item(base, k, 3)
                if it is not None:
                    n, s = it
                    act.wait_ge(idx_ps, n + 1)
                    wait(act, pv_rdy, n - R + 1)
                    nc.scalar.activation(idx[:, s, :], ps_idx[:, 0:SUB], ACT.Copy).then_inc(idx_rdy, 1)
                    nc.scalar.activation(rel[:, s, :], ps_idx[:, SUB:2 * SUB], ACT.Identity,
                                         bias=keep.minus_first[:, bass.ds(n, 1)])
                    wait(act, msel_ps, n - R + 1)
                    nc.scalar.activation(sel[:, s, :, HEADS], ps_idx[:, 2 * SUB:3 * SUB], ACT.Identity,
                                         bias=keep.lastcol[:, 0:1], scale=keep.notlast[:, 0:1]).then_inc(rel_rdy, 1)
                it = item(base, k, 2)
                if it is not None:
                    n, s = it
                    act.wait_ge(rel_rdy, n + 1)
                    wait(act, oh_rdy, n)
                    for g in range(SUB):
                        last = nc.scalar.activation(sq[:, g, :], keep.iota[:, :], ACT.Square, bias=rel[:, s, g:g + 1], scale=-1.0)
                    last.then_inc(sq_rdy, 1)
                    act.wait_ge(sq_rdy, n + 1)
                    wait(act, ohT_ps, n - 1)
                    wait(act, oh32_rdy, n - 1)
                    nc.scalar.activation(oh16[:, s % 2, :, :], sq[:, :, :], ACT.Relu, bias=keep.ones[:, 0:1],
                                         scale=-2.0).then_inc(oh_rdy, 1)
                    act.wait_ge(oh_rdy, n + 1)
                    wait(act, agg_ps, n - R + 1)
                    nc.scalar.activation(oh32[:, s, :, :], oh16[:, s % 2, :, :], ACT.Copy).then_inc(oh32_rdy, 1)
            pipeline(act, go)

        @block.tensor
        def _(pe):
            def sums(it, tiles):
                n, s = it
                if tiles[0] == 0:
                    pe.wait_ge(pv_rdy, n + 1)
                    wait(pe, acc_rdy, n - 1)
                for g in tiles:
                    mm = nc.tensor.matmul(ps_agg[s % 2][:, 0:FA], oh32[:, s, g, :], pv[:, s % 2, g, :],
                                          start=(g == 0), stop=(g == SUB - 1))
                if tiles[-1] == SUB - 1:
                    mm.then_inc(agg_ps, 1)

            def q_rows(it, half, w):
                n, s = it
                if half == 0:
                    pe.wait_ge(ohT_rdy, n + 1)
                    wait(pe, prod_rdy, n)
                for g in (2 * half, 2 * half + 1):
                    mm = nc.tensor.matmul(ps_q[:, g * F:(g + 1) * F], ohT[:, s, g, :],
                                          keep.q[:, bass.ds(w * F, F)], start=True, stop=True)
                if half == 1:
                    mm.then_inc(q_ps, 1)

            def go(base, k):
                it = item(base, k, -1)
                if it is not None:
                    n, s = it
                    wait_apart(pe, pe_passed, (run_rdy, n + 1))
                    nc.tensor.transpose(ps_s[:, 128:128 + SUB * HEADS], run[:, s, :],
                                        keep.ident[0:SUB * HEADS, 0:SUB * HEADS]).then_inc(back_ps, 1)
                agg_it, q_it = item(base, k, -3), item(base, k, 1)
                if agg_it is not None:
                    sums(agg_it, range(SUB - 1))
                if q_it is not None:
                    w = pe.value_load(keep.w_i[0:1, bass.ds(q_it[0], 1)], min_val=0, max_val=z.NT - 1)
                it = item(base, k, -1)
                if it is not None:
                    n, s = it
                    pe.wait_ge(sel_rdy, n + 1)
                    pe.wait_ge(oh32_rdy, n + 1)
                    wait(pe, arg_rdy, n)
                    for g in range(SUB):
                        mm = nc.tensor.matmul(ps_m[:, 9 * g:9 * g + 9], oh32[:, s, g, :], sel[:, s, g, :],
                                              start=True, stop=True)
                    mm.then_inc(msel_ps, 1)
                if agg_it is not None:
                    sums(agg_it, range(SUB - 1, SUB))
                it = item(base, k, 0)
                if it is not None:
                    n, s = it
                    pe.wait_ge(dots_rdy, n + 1)
                    wait(pe, sel_rdy, n)
                    nc.tensor.transpose(ps_s[0:SUB * HEADS, 0:P], score[:, s, :], keep.ident[:, :]).then_inc(eT_ps, 1)
                if q_it is not None:
                    q_rows(q_it, 0, w)
                it = item(base, k, -1)
                if it is not None:
                    n, s = it
                    pe.wait_ge(m_rdy, n + 1)
                    for g in range(SUB):
                        mm = nc.tensor.matmul(ps_m[:, 64 + 8 * g:72 + 8 * g], ohT[:, s, g, :], mnew[:, s, :],
                                              start=True, stop=True)
                    mm.then_inc(me_ps, 1)
                if q_it is not None:
                    q_rows(q_it, 1, w)
                it = item(base, k, 2)
                if it is not None:
                    n, s = it
                    pe.wait_ge(oh_rdy, n + 1)
                    wait(pe, ohT_rdy, n)
                    for g in range(SUB):
                        mm = nc.tensor.transpose(ps_oh[:, g * P:(g + 1) * P], oh16[:, s % 2, g, :], keep.identb[:, :])
                    mm.then_inc(ohT_ps, 1)
                it = item(base, k, 4)
                if it is not None:
                    n, s = it
                    wait_slot(pe, rows_in[s], n, s, LOADS)
                    wait_apart(pe, pe_passed, (rel_rdy, n))
                    nc.tensor.transpose(ps_idx[:, 0:3 * SUB], rows[:, s, :], keep.ident[0:3 * SUB, 0:3 * SUB]).then_inc(idx_ps, 1)
            pipeline(pe, go)

        @block.vector
        def _(dve):
            def go(base, k):
                it = item(base, k, -1)
                if it is not None:
                    n, s = it
                    dve.wait_ge(eT_ps, n + 1)
                    wait_slot(dve, rows_in[s], n, s, LOADS)
                    wait(dve, back_ps, n - R + 1)
                    nc.vector.tensor_tensor_scan(run[:, s, :], pen[:, s, :], ps_s[0:SUB * HEADS, 0:P], -BIG,
                                                 ALU.add, ALU.max).then_inc(run_rdy, 1)
                it = item(base, k, 0)
                if it is not None:
                    n, s = it
                    wait_slot(dve, kv_in[s], n, s, 16 * SUB)
                    dve.wait_ge(q_ps, n + 1)
                    wait(dve, dots_rdy, n)
                    nc.vector.tensor_tensor(prod[:, :, :], kv[:, s, :, 0:F],
                                            ps_q[:, :].rearrange("p (g f) -> p g f", g=SUB), ALU.mult).then_inc(prod_rdy, 1)
                it = item(base, k, -1)
                if it is not None:
                    n, s = it
                    dve.wait_ge(back_ps, n + 1)
                    dve.wait_ge(rel_rdy, n + 1)
                    nc.vector.scalar_tensor_tensor(
                        out=sel[:, s, :, 0:HEADS], in0=sel[:, s, :, HEADS:HEADS + 1].to_broadcast([P, SUB, HEADS]),
                        scalar=1.0 / BIG, in1=ps_s[:, 128:128 + SUB * HEADS].rearrange("p (g h) -> p g h", h=HEADS),
                        op0=ALU.mult, op1=ALU.mult).then_inc(sel_rdy, 1)
                it = item(base, k, 0)
                if it is not None:
                    n, s = it
                    dve.wait_ge(prod_rdy, n + 1)
                    wait(dve, arg_rdy, n - R + 1)
                    nc.vector.tensor_reduce(score[:, s, :], prod[:, :, :].rearrange("p g (h d) -> p (g h) d", d=DH),
                                            AX.X, ALU.add).then_inc(dots_rdy, 1)
                it = item(base, k, -3)
                if it is not None:
                    w_acc = dve.value_load(keep.w_i[0:1, bass.ds(it[0], 1)], min_val=0, max_val=z.NT - 1)
                it = item(base, k, -1)
                if it is not None:
                    n, s = it
                    dve.wait_ge(msel_ps, n + 1)
                    tile_max = ps_m[:, 0:9 * SUB].rearrange("p (g h) -> p g h", h=HEADS + 1)
                    nc.vector.tensor_scalar(absent[:, :], tile_max[:, :, HEADS], -BIG, None, ALU.add).then_inc(m_step, 1)
                    dve.wait_ge(m_step, 4 * n + 1)
                    nc.vector.tensor_tensor(cand[:, :, :], tile_max[:, :, 0:HEADS],
                                            absent[:, :].rearrange("p (g a) -> p g a", a=1).to_broadcast([P, SUB, HEADS]),
                                            ALU.add).then_inc(m_step, 1)
                    dve.wait_ge(m_step, 4 * n + 2)
                    nc.vector.tensor_reduce(top[:, :], cand[:, :, :].rearrange("p g h -> p h g"), AX.X, ALU.max).then_inc(m_step, 1)
                    before = mnew[:, (s - 1) % R, :]
                    reset = keep.reset[:, bass.ds(n, 1)]
                    dve.wait_ge(m_step, 4 * n + 3)
                    wait(dve, m_rdy, n)
                    wait(dve, me_ps, n - R + 1)
                    nc.vector.scalar_tensor_tensor(out=mnew[:, s, :], in0=before, scalar=reset, in1=top[:, :],
                                                   op0=ALU.add, op1=ALU.max).then_inc(m_rdy, 1)
                    dve.wait_ge(m_rdy, n + 1)
                    wait(dve, al_rdy, n - R + 1)
                    nc.vector.scalar_tensor_tensor(out=mdif[:, s, :], in0=before, scalar=reset, in1=mnew[:, s, :],
                                                   op0=ALU.add, op1=ALU.subtract).then_inc(m_step, 1)
                it = item(base, k, -2)
                if it is not None:
                    n, s = it
                    dve.wait_ge(p_rdy, n + 1)
                    wait(dve, agg_ps, n - 1)
                    out = pv[:, s % 2, :, :].rearrange("p g (h c) -> p g h c", c=HC)
                    nc.vector.tensor_tensor(out[:, :, :, 0:DH], kv[:, s, :, F:2 * F].rearrange("p g (h d) -> p g h d", d=DH),
                                            out[:, :, :, DH:HC].to_broadcast([P, SUB, HEADS, DH]), ALU.mult).then_inc(pv_rdy, 1)
                it = item(base, k, -3)
                if it is not None:
                    n, s = it
                    acc = keep.acc[:, bass.ds(w_acc * FA, FA)]
                    dve.wait_ge(al_rdy, n + 1)
                    wait(dve, acc_rdy, n)
                    nc.vector.tensor_tensor(acc.rearrange("p (h c) -> p h c", c=HC), acc.rearrange("p (h c) -> p h c", c=HC),
                                            alpha[:, s, :].rearrange("p (h a) -> p h a", a=1).to_broadcast([P, HEADS, HC]),
                                            ALU.mult).then_inc(acc_half, 1)
                it = item(base, k, -1)
                if it is not None:
                    n, s = it
                    dve.wait_ge(me_ps, n + 1)
                    wait(dve, p_rdy, n - R + 1)
                    nc.vector.tensor_tensor(arg[:, s, :], score[:, s, :], ps_m[:, 64:64 + SUB * HEADS],
                                            ALU.subtract).then_inc(arg_rdy, 1)
                it = item(base, k, -3)
                if it is not None:
                    n, s = it
                    dve.wait_ge(acc_half, n + 1)
                    dve.wait_ge(agg_ps, n + 1)
                    nc.vector.tensor_tensor(acc, acc, ps_agg[s % 2][:, 0:FA], ALU.add).then_inc(acc_rdy, 1)
            nc.vector.memset(mnew[:, R - 1, :], 0.0).then_inc(first_max, 1)
            dve.wait_ge(first_max, 1)
            pipeline(dve, go)


class Turns:

    def __init__(self, first, sizes):
        self.first, self.sizes = first, sizes

    def before(self, b):
        if isinstance(b, int):
            return sum(self.sizes(i) for i in range(self.first, b))
        return b * self.sizes(0) + sum(self.sizes(i) for i in range(self.first, 0))


def ffn_phase(nc, z, w, x, feat_d, out, keep):
    TB, NB, X, H1 = z.TB, z.NB, z.X, z.H1
    M1 = H1 // P
    KC = F // P
    TOK = TB * P
    CH = -(-TOK // 512)
    CW = TOK // CH
    G = -(-TB // 2)
    G += G % 2
    assert NB >= 2 and X == HEADS and TOK % CH == 0 and (M1 * CH) % 4 == 0 and (X * KC * CH) % 4 == 0
    with ExitStack() as ctx:
        def sb(name, shape, dt=F32):
            return ctx.enter_context(nc.sbuf_tensor("f_" + name, shape, dt))

        def sem(name):
            return ctx.enter_context(nc.semaphore("f_" + name))

        def bank(name):
            return ctx.enter_context(nc.psum_tensor(name, [P, 512], F32))

        w1 = sb("w1", [P, KC, H1])
        w2 = sb("w2", [P, M1, F])
        ew1 = sb("ew1", [P, X, KC, F])
        ew2 = sb("ew2", [P, X, KC, F])
        eb2 = sb("eb2", [X, F])
        ln_g = sb("ln_g_rows", [P, F])
        ln_b = sb("ln_b_rows", [P, F])
        b2 = sb("b2_rows", [P, F])
        nrows = 2 * M1 + X * KC
        bias_rows = sb("bias_rows", [nrows, P])
        bias = sb("bias", [P, nrows])
        rt_rows = sb("router_rows", [X, F])
        router = sb("routerT", [P, KC, X])
        feat = sb("feat_in", [P, TB, F])
        r1 = sb("r1", [P, TB, F])
        r1T = sb("r1T", [P, KC, TOK])
        hT = sb("hiddenT", [P, M1, TOK])
        bend = sb("bend", [P, 2, CW])
        side = sb("side", [P, M1])
        rise = sb("rise", [P, M1])
        rise_b = sb("rise_b1", [P, M1])
        slope = sb("side_alpha", [P, M1])
        slope_b = sb("side_alpha_b1", [P, M1])
        h2 = sb("h2", [P, TB, F])
        xo = sb("x_out", [P, TB, F])
        t = sb("tokens", [P, TB, F])
        tT = sb("tokensT", [P, KC, TOK])
        den = sb("den", [P, TB * HEADS])
        stats = sb("stats", [P, TB, 6])
        mv = sb("mv", [P, TB, 2])
        var = sb("var", [P, TB])
        rstd = sb("rstd", [P, TB])
        tmp = sb("tmp", [P, TB])
        prob = sb("prob", [P, TB, X])
        pick = sb("pick", [P, 3, TB, X])
        best = sb("best", [P, 2, TB])
        comb = sb("comb", [P, TB, X])
        combT = sb("combT", [X, TOK])

        ps_h = [bank(f"ps_h{i}") for i in range(4)]
        ps_y = [bank(f"ps_y{i}") for i in range(2)]
        ps_t = [bank(f"ps_t{i}") for i in range(2)]

        w_in = sem("weights_loaded")
        feat_in = sem("feat_loaded")
        x_in = sem("x_loaded")
        out_st = sem("out_stored")
        dvec = sem("dve_step")
        passed = sem("dve_passed")
        setup_ps = sem("setup_in_psum")
        setup_rdy = sem("setup_ready")
        r1_rdy = sem("r1_ready")
        t_rdy = sem("tokens_ready")
        tr_ps = sem("transposed_in_psum")
        tr_rdy = sem("transposed_ready")
        h_ps = sem("hidden_in_psum")
        h_rdy = sem("hidden_ready")
        prelu_rdy = sem("prelu_ready")
        y_ps = sem("rows_in_psum")
        y_rdy = sem("rows_taken")
        rows_done = sem("block_rows_done")
        lg_rdy = sem("logits_less_max")
        pe_rdy = sem("exp_ready")
        zero_rdy = sem("x_zeroed")

        spots = [[] for _ in range(X)]
        for j in range(TB):
            spots[min(X - 1, X - 5 + (j + 1) // 2 + (0 if j else 0))].append(j)

        has_ffn = lambda b: isinstance(b, int) and -1 <= b <= NB - 2 or not isinstance(b, int)
        has_moe = lambda b: not isinstance(b, int) or 0 <= b
        has_pre = lambda b: not isinstance(b, int) or b <= NB - 3
        y_turn = Turns(-2, lambda b: G * (has_ffn(b) + (1 + X) * has_moe(b)))
        h_turn = Turns(-2, lambda b: CH * (M1 * has_ffn(b) + X * KC * has_moe(b)))
        t_turn = Turns(-2, lambda b: (TB + 1 + 2) * has_moe(b) + TB * has_pre(b))

        def iterations(eng, body):
            body(-2)
            body(-1)
            if NB > 2:
                with eng.Fori(0, NB - 2) as b:
                    body(b)
            body(NB - 2)
            body(NB - 1)

        def wait(eng, s, value):
            if not (isinstance(value, int) and value <= 0):
                eng.wait_ge(s, value)

        xb = x[0:(z.NT - 1) * P, :].rearrange("(t p) f -> p t f", p=P)
        ob = out[0:(z.NT - 1) * P, :].rearrange("(t p) f -> p t f", p=P)
        featb = feat_d.rearrange("(t p) f -> p t f", p=P)
        block = ctx.enter_context(nc.Block())

        def groups():
            tiles = [list(range(i, min(i + 2, TB))) for i in range(0, TB, 2)]
            while len(tiles) < G:
                big = max(tiles, key=len)
                at = tiles.index(big)
                tiles[at:at + 1] = [big[:1], big[1:]] if len(big) > 1 else [big, []]
            return tiles

        GROUPS = groups()

        @block.sync
        def _(sp):
            first = [(w1[:, :, :], w.W1.rearrange("(c p) n -> p c n", p=P)),
                     (w2[:, :, :], w.W2.rearrange("(c p) n -> p c n", p=P)),
                     (bias_rows[0:M1, :], w.b1.rearrange("(m p) -> m p", p=P)),
                     (bias_rows[M1:2 * M1, :], w.alpha.rearrange("(m p) -> m p", p=P)),
                     (bias_rows[2 * M1:nrows, :], w.eb1.rearrange("e (c p) -> (e c) p", p=P)),
                     (rt_rows[:, :], w.router),
                     (eb2[:, :], w.eb2)]
            first += [(o[:, :], v.rearrange("(a n) -> a n", a=1).to_broadcast([P, F]))
                      for o, v in ((ln_g, w.ln_g), (ln_b, w.ln_b), (b2, w.b2))]
            for e in range(X):
                first += [(ew1[:, e, :, :], w.ew1[e].rearrange("(c p) n -> p c n", p=P)),
                          (ew2[:, e, :, :], w.ew2[e].rearrange("(c p) n -> p c n", p=P))]
            sp.dma_start(feat[:, :, :], featb[:, 0:TB, :]).then_inc(feat_in, 16)
            for o, v in first:
                sp.dma_start(o, v).then_inc(w_in, 16)

            def body(b):
                if has_pre(b) and not (isinstance(b, int) and b == -2):
                    sp.wait_ge(r1_rdy, b + 2)
                    sp.dma_start(feat[:, :, :], featb[:, bass.ds((b + 2) * TB, TB), :]).then_inc(feat_in, 16)
                if has_moe(b):
                    wait(sp, out_st, 16 * b)
                    if isinstance(b, int) and b == 0:
                        sp.wait_ge(zero_rdy, 1)
                    if isinstance(b, int) and b == NB - 1:
                        sp.dma_start(xo[0:z.tail, TB - 1, :], x[(z.NT - 1) * P:z.N, :]).then_inc(x_in, 16)
                        sp.dma_start(xo[:, 0:TB - 1, :], xb[:, b * TB:b * TB + TB - 1, :]).then_inc(x_in, 16)
                    else:
                        if not isinstance(b, int):
                            sp.wait_ge(zero_rdy, 1)
                        sp.dma_start(xo[:, :, :], xb[:, bass.ds(b * TB, TB), :]).then_inc(x_in, 32)
                    sp.wait_ge(rows_done, b + 1)
                    if isinstance(b, int) and b == NB - 1:
                        sp.dma_start(ob[:, b * TB:b * TB + TB - 1, :], xo[:, 0:TB - 1, :]).then_inc(out_st, 16)
                        sp.dma_start(out[(z.NT - 1) * P:z.N, :], xo[0:z.tail, TB - 1, :]).then_inc(out_st, 16)
                    else:
                        sp.dma_start(ob[:, bass.ds(b * TB, TB), :], xo[:, :, :]).then_inc(out_st, 16)
            iterations(sp, body)
            sp.wait_ge(out_st, 16 * (NB + 1))

        @block.tensor
        def _(pe):
            pe.wait_ge(w_in, 16 * (10 + 2 * X))
            nc.tensor.transpose(ps_t[0][:, 0:nrows], bias_rows[:, :], keep.ident[0:nrows, 0:nrows])
            for c in range(KC):
                mm = nc.tensor.transpose(ps_t[0][:, 64 + c * X:64 + (c + 1) * X], rt_rows[:, c * P:(c + 1) * P],
                                         keep.ident[0:X, 0:X])
            mm.then_inc(setup_ps, 1)
            pe.wait_ge(setup_rdy, 1)

            def ffn(b):
                u = h_turn.before(b)
                pe.wait_ge(tr_rdy, t_turn.before(b))
                i = 0
                for m in range(M1):
                    for c in range(CH):
                        wait(pe, h_rdy, u + i - 3)
                        for k in range(KC):
                            mm = nc.tensor.matmul(ps_h[i % 4][:, 0:CW], w1[:, k, m * P:(m + 1) * P],
                                                  r1T[:, k, c * CW:(c + 1) * CW], start=(k == 0), stop=(k == KC - 1))
                        mm.then_inc(h_ps, 1)
                        i += 1
                pe.wait_ge(prelu_rdy, M1 * CH * (b + 2))
                rows(y_turn.before(b), [(hT[:, m, :], w2[:, m, :]) for m in range(M1)])

            def rows(u, terms):
                for g, tiles in enumerate(GROUPS):
                    wait(pe, y_rdy, u + g - 1)
                    for i, j in enumerate(tiles):
                        for n, (lhs, rhs) in enumerate(terms):
                            mm = nc.tensor.matmul(ps_y[g % 2][:, i * F:(i + 1) * F], lhs[:, j * P:(j + 1) * P], rhs,
                                                  start=(n == 0), stop=(n == len(terms) - 1))
                    mm.then_inc(y_ps, 1)

            def turn_rows(src_, j, bank_, u, all_before):
                wait(pe, tr_rdy, u if all_before else u - 1)
                for c in range(KC):
                    mm = nc.tensor.transpose(ps_t[bank_][:, c * P:(c + 1) * P], src_[:, j, c * P:(c + 1) * P],
                                             keep.ident[:, :])
                mm.then_inc(tr_ps, 1)

            def expert_hidden(b, e):
                u = h_turn.before(b) + CH * (M1 if has_ffn(b) else 0) + e * KC * CH
                i = 0
                for m in range(KC):
                    for c in range(CH):
                        wait(pe, h_rdy, u + i - 3)
                        for k in range(KC):
                            mm = nc.tensor.matmul(ps_h[i % 4][:, 0:CW], ew1[:, e, k, m * P:(m + 1) * P],
                                                  tT[:, k, c * CW:(c + 1) * CW], start=(k == 0), stop=(k == KC - 1))
                        mm.then_inc(h_ps, 1)
                        i += 1

            def expert_rows(b, e):
                pe.wait_ge(h_rdy, h_turn.before(b) + CH * (M1 if has_ffn(b) else 0) + (e + 1) * KC * CH)
                s = e % 2
                u = y_turn.before(b) + G * ((1 if has_ffn(b) else 0) + (0 if e == 0 else 1) + e)
                rows(u, [(hT[:, 2 * s + m, :], ew2[:, e, m, :]) for m in range(KC)])

            def body(b):
                if has_ffn(b):
                    ffn(b)
                u = t_turn.before(b)
                if has_moe(b):
                    pe.wait_ge(t_rdy, b + 1)
                    for j in range(TB):
                        turn_rows(t, j, j % 2, u + j, j == 0)
                    pe.wait_ge(tr_rdy, u + TB)
                    for j in range(TB):
                        for k in range(KC):
                            mm = nc.tensor.matmul(ps_t[1][:, j * X:(j + 1) * X], tT[:, k, j * P:(j + 1) * P],
                                                  router[:, k, :], start=(k == 0), stop=(k == KC - 1))
                    mm.then_inc(tr_ps, 1)
                    expert_hidden(b, 0)
                    for e in range(X):
                        if e + 1 < X:
                            expert_hidden(b, e + 1)
                        expert_rows(b, e)
                        if e == 0:
                            pe.wait_ge(lg_rdy, 2 * (b + 1))
                            for i, tiles in enumerate((range(0, TB // 2), range(TB // 2, TB))):
                                wait(pe, tr_rdy, u + TB + 1 + i)
                                for n, j in enumerate(tiles):
                                    mm = nc.tensor.transpose(ps_t[i][0:X, n * P:(n + 1) * P], comb[:, j, :], keep.ident[:, :])
                                mm.then_inc(tr_ps, 1)
                            pe.wait_ge(tr_rdy, u + TB + 3)
                            rows(y_turn.before(b) + G * ((1 if has_ffn(b) else 0) + 1), [(combT[:, :], eb2[:, :])])
                        if has_pre(b):
                            for j in spots[e]:
                                if j == 0:
                                    pe.wait_ge(r1_rdy, b + 3)
                                turn_rows(r1, j, j % 2, u + TB + 3 + j, j == 0)
                elif has_pre(b):
                    pe.wait_ge(r1_rdy, b + 3)
                    for j in range(TB):
                        turn_rows(r1, j, j % 2, u + j, j == 0)
            iterations(pe, body)

        @block.scalar
        def _(act):
            act.wait_ge(setup_rdy, 1)

            def r1_evac(b, j, u):
                act.wait_ge(tr_ps, u + 1)
                nc.scalar.activation(r1T[:, :, j * P:(j + 1) * P],
                                     ps_t[j % 2][:, 0:KC * P].rearrange("p (c n) -> p c n", c=KC), ACT.Copy).then_inc(tr_rdy, 1)

            def hidden(b, e):
                u = h_turn.before(b) + CH * (M1 if has_ffn(b) else 0) + e * KC * CH
                s = e % 2
                if e < 2:
                    wait(act, y_ps, y_turn.before(b) + (G if has_ffn(b) else 0))
                else:
                    act.wait_ge(y_ps, y_turn.before(b) + G * ((1 if has_ffn(b) else 0) + (1 if e > 2 else 0) + e - 1))
                i = 0
                for m in range(KC):
                    for c in range(CH):
                        act.wait_ge(h_ps, u + i + 1)
                        nc.scalar.activation(hT[:, 2 * s + m, c * CW:(c + 1) * CW], ps_h[i % 4][:, 0:CW], ACT.Gelu,
                                             bias=bias[:, 2 * M1 + e * KC + m:2 * M1 + e * KC + m + 1]).then_inc(h_rdy, 1)
                        i += 1

            def body(b):
                if has_ffn(b):
                    u = h_turn.before(b)
                    v = M1 * CH * (b + 1)
                    wait(act, y_ps, y_turn.before(b))
                    i = 0
                    for m in range(M1):
                        for c in range(CH):
                            act.wait_ge(h_ps, u + i + 1)
                            nc.scalar.activation(hT[:, m, c * CW:(c + 1) * CW], ps_h[i % 4][:, 0:CW], ACT.Relu,
                                                 bias=rise_b[:, m:m + 1], scale=rise[:, m:m + 1])
                            wait(act, prelu_rdy, v + i - 1)
                            nc.scalar.activation(bend[:, i % 2, :], ps_h[i % 4][:, 0:CW], ACT.Identity,
                                                 bias=slope_b[:, m:m + 1], scale=slope[:, m:m + 1]).then_inc(h_rdy, 1)
                            i += 1
                u = t_turn.before(b)
                if has_moe(b):
                    act.wait_ge(lg_rdy, 2 * b + 1)
                    nc.scalar.activation(prob[:, :, :], prob[:, :, :], ACT.Exp).then_inc(pe_rdy, 1)
                    hidden(b, 0)
                    for e in range(X):
                        if e + 1 < X:
                            hidden(b, e + 1)
                        if has_pre(b):
                            for j in spots[e]:
                                r1_evac(b, j, u + TB + 3 + j)
                elif has_pre(b):
                    for j in range(TB):
                        r1_evac(b, j, u + j)
            iterations(act, body)

        @block.gpsimd
        def _(pool):
            pool.wait_ge(setup_rdy, 1)

            def body(b):
                if not has_ffn(b):
                    return
                u = h_turn.before(b)
                i = 0
                for m in range(M1):
                    for c in range(CH):
                        h = hT[:, m, c * CW:(c + 1) * CW]
                        pool.wait_ge(h_rdy, u + i + 1)
                        nc.gpsimd.tensor_tensor(h, h, bend[:, i % 2, :], ALU.add).then_inc(prelu_rdy, 1)
                        i += 1
            iterations(pool, body)

        @block.vector
        def _(dve):
            step = Chain(dve, dvec)

            def norm(src_, dst_, affine):
                for j in range(TB):
                    last = nc.vector.bn_stats(stats[:, j, :], src_[:, j, :])
                step(last, apart=passed)
                for j in range(TB):
                    last = nc.vector.bn_aggr(mv[:, j, :], stats[:, j, :])
                step(last)
                step(nc.vector.tensor_scalar(var[:, :], mv[:, :, 1], EPS, None, ALU.add))
                rsqrt(nc, step, var[:, :], rstd[:, :], tmp[:, :])
                for j in range(TB):
                    last = nc.vector.tensor_scalar(dst_[:, j, :], src_[:, j, :], mv[:, j, 0:1], rstd[:, j:j + 1],
                                                   ALU.subtract, ALU.mult)
                if affine:
                    step(last)
                    step(nc.vector.tensor_tensor(dst_[:, :, :], dst_[:, :, :], over_tiles(ln_g), ALU.mult))
                    last = nc.vector.tensor_tensor(dst_[:, :, :], dst_[:, :, :], over_tiles(ln_b), ALU.add)
                return last

            def over_tiles(rows_):
                return rows_[:, :].rearrange("p (a f) -> p a f", a=1).to_broadcast([P, TB, F])

            def pre(b):
                c = b + 2
                a = keep.acc[:, bass.ds(c * (TB * FA), TB * FA)].rearrange("p (n c) -> p n c", c=HC)
                step(nc.vector.tensor_scalar(den[:, :], a[:, :, DH], 1e-30, None, ALU.max))
                step(nc.vector.reciprocal(den[:, :], den[:, :]))
                r = r1[:, :, :].rearrange("p t (h d) -> p (t h) d", d=DH)
                step(nc.vector.tensor_tensor(r, a[:, :, 0:DH], den[:, :].rearrange("p (n a) -> p n a", a=1).to_broadcast(
                    [P, TB * HEADS, DH]), ALU.mult))
                dve.wait_ge(feat_in, 16 * (c + 1))
                step(nc.vector.tensor_tensor(r1[:, :, :], r1[:, :, :], feat[:, :, :], ALU.add))
                norm(r1, r1, True).then_inc(r1_rdy, 1)

            def pick_best():
                step(nc.vector.tensor_reduce(best[:, 0, :], pick[:, 0, :, :], AX.X, ALU.max))
                step(nc.vector.tensor_tensor(pick[:, 1, :, :], pick[:, 0, :, :], of_tile(best[:, 0, :]), ALU.is_equal))
                step(nc.vector.tensor_tensor(pick[:, 1, :, :], pick[:, 1, :, :], order(), ALU.mult))
                step(nc.vector.tensor_reduce(best[:, 1, :], pick[:, 1, :, :], AX.X, ALU.max))
                step(nc.vector.tensor_tensor(pick[:, 2, :, :], order(), of_tile(best[:, 1, :]), ALU.is_equal))

            def of_tile(v):
                return v.rearrange("p (t a) -> p t a", a=1).to_broadcast([P, TB, X])

            def order():
                return keep.iota8[:, :].rearrange("p (a x) -> p a x", a=1).to_broadcast([P, TB, X])

            def body(b):
                ut, uy = t_turn.before(b), y_turn.before(b)
                if has_moe(b):
                    step(norm(h2, h2, True))
                    dve.wait_ge(x_in, 32 * (b + 1))
                    step(nc.vector.tensor_tensor(xo[:, :, :], xo[:, :, :], h2[:, :, :], ALU.add))
                    step(norm(xo, t, False))
                    step(nc.vector.tensor_tensor(xo[:, :, :], xo[:, :, :], t[:, :, :], ALU.add))
                    nc.vector.tensor_copy(best[:, 0, 0:1], best[:, 0, 0:1]).then_inc(t_rdy, 1)
                if has_ffn(b):
                    dve.wait_ge(tr_rdy, ut)
                    step(nc.vector.tensor_tensor(r1[:, :, :], r1[:, :, :], over_tiles(b2), ALU.add))
                    for g, tiles in enumerate(GROUPS):
                        dve.wait_ge(y_ps, uy + g + 1)
                        n = len(tiles)
                        j = tiles[0]
                        nc.vector.tensor_tensor(h2[:, j:j + n, :], ps_y[g % 2][:, 0:n * F].rearrange("p (n f) -> p n f", n=n),
                                                r1[:, j:j + n, :], ALU.add).then_inc(y_rdy, 1)
                    dve.wait_ge(y_rdy, uy + G)
                if has_moe(b):
                    for j in range(TB):
                        dve.wait_ge(tr_ps, ut + j + 1)
                        nc.vector.tensor_copy(tT[:, :, j * P:(j + 1) * P],
                                              ps_t[j % 2][:, 0:KC * P].rearrange("p (c n) -> p c n", c=KC)).then_inc(tr_rdy, 1)
                    dve.wait_ge(tr_ps, ut + TB + 1)
                    lg = ps_t[1][:, 0:TB * X].rearrange("p (t x) -> p t x", x=X)
                    step(nc.vector.tensor_reduce(best[:, 0, :], lg, AX.X, ALU.max))
                    ins = nc.vector.tensor_tensor(prob[:, :, :], lg, of_tile(best[:, 0, :]), ALU.subtract)
                    ins.then_inc(tr_rdy, 1)
                    dve.wait_ge(tr_rdy, ut + TB + 1)
                    nc.vector.tensor_copy(best[:, 1, 0:1], best[:, 0, 0:1]).then_inc(lg_rdy, 1)
                    dve.wait_ge(pe_rdy, b + 1)
                    step(nc.vector.tensor_reduce(best[:, 0, :], prob[:, :, :], AX.X, ALU.add))
                    step(nc.vector.reciprocal(best[:, 0, :], best[:, 0, :]))
                    step(nc.vector.tensor_tensor(prob[:, :, :], prob[:, :, :], of_tile(best[:, 0, :]), ALU.mult))
                    step(nc.vector.tensor_copy(pick[:, 0, :, :], prob[:, :, :]))
                    pick_best()
                    step(nc.vector.scalar_tensor_tensor(out=pick[:, 0, :, :], in0=pick[:, 2, :, :], scalar=-2.0,
                                                        in1=prob[:, :, :], op0=ALU.mult, op1=ALU.add))
                    step(nc.vector.tensor_tensor(comb[:, :, :], pick[:, 2, :, :], prob[:, :, :], ALU.mult))
                    pick_best()
                    step(nc.vector.tensor_tensor(pick[:, 2, :, :], pick[:, 2, :, :], prob[:, :, :], ALU.mult))
                    step(nc.vector.tensor_tensor(comb[:, :, :], comb[:, :, :], pick[:, 2, :, :], ALU.add))
                    step(nc.vector.tensor_reduce(best[:, 0, :], comb[:, :, :], AX.X, ALU.add))
                    step(nc.vector.tensor_scalar(best[:, 0, :], best[:, 0, :], 1e-12, None, ALU.max))
                    step(nc.vector.reciprocal(best[:, 0, :], best[:, 0, :]))
                    nc.vector.tensor_tensor(comb[:, :, :], comb[:, :, :], of_tile(best[:, 0, :]), ALU.mult).then_inc(lg_rdy, 1)
                    dve.wait_ge(lg_rdy, 2 * (b + 1))
                    base = uy + (G if has_ffn(b) else 0)

                    def experts_share(e, at):
                        for g, tiles in enumerate(GROUPS):
                            dve.wait_ge(y_ps, at + g + 1)
                            for i, j in enumerate(tiles):
                                last = nc.vector.scalar_tensor_tensor(
                                    out=xo[:, j, :], in0=ps_y[g % 2][:, i * F:(i + 1) * F], scalar=comb[:, j, e:e + 1],
                                    in1=xo[:, j, :], op0=ALU.mult, op1=ALU.add)
                            last.then_inc(y_rdy, 1)
                        dve.wait_ge(y_rdy, at + G)

                    for e in range(X):
                        experts_share(e, base + G * (e + (0 if e == 0 else 1)))
                        if e == 0:
                            for i, tiles in enumerate((range(0, TB // 2), range(TB // 2, TB))):
                                dve.wait_ge(tr_ps, ut + TB + 2 + i)
                                n = len(tiles) * P
                                nc.vector.tensor_copy(combT[:, tiles[0] * P:tiles[0] * P + n], ps_t[i][0:X, 0:n]).then_inc(tr_rdy, 1)
                            for g, tiles in enumerate(GROUPS):
                                dve.wait_ge(y_ps, base + G + g + 1)
                                n, j = len(tiles), tiles[0]
                                nc.vector.tensor_tensor(xo[:, j:j + n, :],
                                                        ps_y[g % 2][:, 0:n * F].rearrange("p (n f) -> p n f", n=n),
                                                        xo[:, j:j + n, :], ALU.add).then_inc(y_rdy, 1)
                            dve.wait_ge(y_rdy, base + 2 * G)
                        if e == 1 and has_pre(b):
                            pre(b)
                    nc.vector.tensor_copy(best[:, 0, 0:1], best[:, 0, 0:1]).then_inc(rows_done, 1)
                elif has_pre(b):
                    pre(b)

            nc.vector.memset(xo[:, :, :], 0.0).then_inc(zero_rdy, 1)
            step(nc.vector.memset(best[:, :, :], 0.0))
            dve.wait_ge(setup_ps, 1)
            step(nc.vector.tensor_copy(bias[:, :], ps_t[0][:, 0:nrows]))
            step(nc.vector.tensor_scalar(side[:, :], bias[:, M1:2 * M1], 1.0, 2.0, ALU.is_le, ALU.mult))
            step(nc.vector.tensor_scalar(side[:, :], side[:, :], -1.0, None, ALU.add))
            step(nc.vector.tensor_tensor(slope[:, :], side[:, :], bias[:, M1:2 * M1], ALU.mult))
            step(nc.vector.tensor_tensor(rise[:, :], side[:, :], slope[:, :], ALU.subtract))
            step(nc.vector.tensor_tensor(rise_b[:, :], rise[:, :], bias[:, 0:M1], ALU.mult))
            step(nc.vector.tensor_tensor(slope_b[:, :], slope[:, :], bias[:, 0:M1], ALU.mult))
            for m in range(M1):
                last = nc.vector.tensor_scalar(w2[:, m, :], w2[:, m, :], side[:, m:m + 1], None, ALU.mult)
            step(last)
            nc.vector.tensor_copy(router[:, :, :], ps_t[0][:, 64:64 + KC * X].rearrange("p (c x) -> p c x", x=X)).then_inc(setup_rdy, 1)
            dve.wait_ge(w_in, 16 * (10 + 2 * X))
            body(-2)
            body(-1)
            if NB > 2:
                start = step.k
                with dve.Fori(0, NB - 2) as b:
                    step.base, step.k = b * STEPS + start, 0
                    body(b)
                assert step.k == STEPS, step.k
                step.base, step.k = start + (NB - 2) * STEPS, 0
            body(NB - 2)
            body(NB - 1)


class Keep:
    pass


def build(nc, x, src, dst, Wq, Wk, Wv, ln_g, ln_b, W1, b1, alpha, W2, b2, router, ew1, eb1, ew2, eb2, out, stop=None):
    z = Sizes(x.shape[0], src.shape[0], W1.shape[1], router.shape[0])
    feat_d = nc.dram_tensor("feat_scratch", (z.NT * P, F), F32, kind="ExternalOutput" if stop else "Internal").ap()
    kv_d = nc.dram_tensor("kv_scratch", (z.NT * P, 2 * F), F32, kind="ExternalOutput" if stop else "Internal").ap()
    etab_d = nc.dram_tensor("edge_scratch", (3, z.EP), F32, kind="ExternalOutput" if stop else "Internal").ap()
    pen_d = nc.dram_tensor("pen_scratch", (z.EP + 1,), F32, kind="ExternalOutput" if stop else "Internal").ap()
    with ExitStack() as ctx:
        keep = Keep()

        def sb(name, shape, dt=F32):
            return ctx.enter_context(nc.sbuf_tensor(name, shape, dt))

        keep.acc = sb("acc", [P, z.NT * FA])
        keep.ident = sb("ident", [P, P])
        keep.identb = sb("identb", [P, P], BF16)
        keep.ones = sb("ones", [P, P])
        keep.iota = sb("iota", [P, P], BF16)
        keep.iota8 = sb("iota8", [P, HEADS])
        keep.lastcol = sb("lastcol", [P, 1])
        keep.notlast = sb("notlast", [P, 1])
        with ExitStack() as ctx2:
            def sb2(name, shape, dt=F32):
                return ctx2.enter_context(nc.sbuf_tensor(name, shape, dt))
            keep.q = sb2("q", [P, z.NT * F])
            keep.reset = sb2("reset", [P, z.NI])
            keep.w_i = sb2("w_i", [P, z.NI], I32)
            keep.e_i = sb2("e_i", [P, z.NI], I32)
            keep.minus_first = sb2("minus_first", [P, z.NI])
            node_phase(nc, z, x, src, dst, Wq, Wk, Wv, feat_d, kv_d, etab_d, pen_d, keep)
            edge_phase(nc, z, kv_d, etab_d, pen_d, keep)
        w = Keep()
        w.W1, w.b1, w.alpha, w.W2, w.b2, w.ln_g, w.ln_b = W1, b1, alpha, W2, b2, ln_g, ln_b
        w.router, w.ew1, w.eb1, w.ew2, w.eb2 = router, ew1, eb1, ew2, eb2
        ffn_phase(nc, z, w, x, feat_d, out, keep)
        if stop:
            with ExitStack() as c3:
                s = c3.enter_context(nc.semaphore("dbg"))
                accd = nc.dram_tensor("acc_dbg", (P, z.NT * FA), F32, kind="ExternalOutput").ap()
                blk = c3.enter_context(nc.Block())

                @blk.sync
                def _(sp):
                    sp.dma_start(accd, keep.acc[:, :]).then_inc(s, 16)
                    sp.wait_ge(s, 16)


_INS = ["x", "src", "dst", "L0_gnn_Wq", "L0_gnn_Wk", "L0_gnn_Wv", "L0_gnn_ln_g", "L0_gnn_ln_b", "L0_gnn_W1", "L0_gnn_b1",
        "L0_gnn_prelu_alpha", "L0_gnn_W2", "L0_gnn_b2", "L0_ffn_router_w", "L0_ffn_w1", "L0_ffn_b1", "L0_ffn_w2", "L0_ffn_b2"]
STOP = None


def kernel(**inputs):
    import numpy as _np
    import concourse.bacc as _bacc
    from concourse import mybir as _mybir
    from concourse.bass_utils import run_bass_kernel_spmd as _run

    nc = _bacc.Bacc("TRN2", target_bir_lowering=False, num_devices=1)
    arrays, args = {}, []
    for name in _INS:
        a = _np.ascontiguousarray(inputs[name])
        arrays[f"in_{name}_dram"] = a
        args.append(nc.dram_tensor(f"in_{name}_dram", a.shape, _mybir.dt.from_np(a.dtype), kind="ExternalInput").ap())
    out = nc.dram_tensor("out_0_dram", inputs["x"].shape, F32, kind="ExternalOutput").ap()
    build(nc, *args, out, stop=STOP)
    r = _run(nc, [arrays], core_ids=[0])
    return r.results[0]["out_0_dram"]
```

```python
from contextlib import ExitStack

import concourse.bass as bass
from concourse import mybir

ALU = mybir.AluOpType
ACT = mybir.ActivationFunctionType
AX = mybir.AxisListType
F32 = mybir.dt.float32
F32R = mybir.dt.float32r
BF16 = mybir.dt.bfloat16
I32 = mybir.dt.int32

P = 128
SUB = 4
ITEM = P * SUB
RING = 6
LAG = 3
QR = 3
HEADS = 8
DH = 32
F = HEADS * DH
HC = DH + 1
FA = HEADS * HC
BIG = 2.0 ** 125
STEPS = 77
EPS = 1e-5


class Sizes:

    def __init__(self, nodes, edges, hidden, experts):
        self.N, self.E, self.H1, self.X = nodes, edges, hidden, experts
        self.NT = -(-nodes // P)
        self.TB = max(b for b in range(1, 8) if self.NT % b == 0)
        self.NB = self.NT // self.TB
        self.tail = nodes - (self.NT - 1) * P
        self.NI = edges // ITEM + self.NT
        self.L = -(-(edges + ITEM) // P)
        self.EP = P * self.L
        self.PAD = self.NT * P + 1024
        assert 4 * RING <= self.NI <= 512 and self.NT + 1 <= P and nodes % P


def affine_identity(nc, pool, tile, size, zeroed, done):
    nc.gpsimd.memset(tile, 0.0).then_inc(zeroed, 1)
    pool.wait_ge(zeroed, 1)
    nc.gpsimd.affine_select(out=tile, in_=tile, compare_op=ALU.not_equal, fill=1.0, base=0,
                            pattern=[[-1, size]], channel_multiplier=1).then_inc(done, 1)


def rsqrt(nc, step, var, rstd, tmp):
    step(nc.vector.tensor_scalar(tmp.bitcast(I32), var.bitcast(I32), 1, None, ALU.logical_shift_right))
    step(nc.vector.tensor_scalar(rstd.bitcast(I32), tmp.bitcast(I32), -1.0, float(0x5F3759DF), ALU.mult, ALU.add))
    for _ in range(3):
        step(nc.vector.tensor_tensor(tmp, rstd, rstd, ALU.mult))
        step(nc.vector.scalar_tensor_tensor(out=tmp, in0=tmp, scalar=-0.5, in1=var, op0=ALU.mult, op1=ALU.mult))
        step(nc.vector.scalar_tensor_tensor(out=rstd, in0=tmp, scalar=1.5, in1=rstd, op0=ALU.add, op1=ALU.mult))


class Chain:

    def __init__(self, eng, sem):
        self.eng, self.sem, self.k, self.base = eng, sem, 0, 0

    def __call__(self, ins, apart=None):
        ins.then_inc(self.sem, 1)
        self.k += 1
        self.eng.wait_ge(self.sem, self.base + self.k)
        if apart is not None:
            self.eng.sem_inc(apart, 1)


def node_phase(nc, z, x, src, dst, Wq, Wk, Wv, feat_d, kv_d, etab_d, pen_d, keep):
    TB, NB, L = z.TB, z.NB, z.L
    with ExitStack() as ctx:
        def sb(name, shape, dt=F32):
            return ctx.enter_context(nc.sbuf_tensor("n_" + name, shape, dt))

        def sem(name):
            return ctx.enter_context(nc.semaphore("n_" + name))

        w_sb = sb("w_qkv", [P, 2, 3 * F])
        x_sb = sb("x_in", [P, TB, F])
        feat = sb("feat", [P, TB, F])
        featT = sb("featT", [P, 2, 2, P])
        kv_out = sb("kv_out", [P, TB, 2 * F])
        stats = sb("stats", [P, TB, 6])
        mv = sb("mv", [P, TB, 2])
        var = sb("var", [P, TB])
        rstd = sb("rstd", [P, TB])
        tmp = sb("tmp", [P, TB])
        idx_i = sb("idx_i", [P, L], I32)
        src_f = sb("src_f", [P, L])
        dst_f = sb("dst_f", [P, L])
        nxt_f = sb("nxt_f", [P, L])
        dst_tile = sb("dst_tile", [P, L], BF16)
        tile_no = sb("tile_no", [P, z.NT + 1])
        junk = sb("junk", [P, L], BF16)
        below = sb("below", [P, z.NT + 1])
        thr = sb("thr", [P, z.E // ITEM + 2])
        junk2 = sb("junk2", [P, z.E // ITEM + 2])
        item_no = sb("item_no", [P, z.NI])
        tri = sb("tri", [P, P])
        seg = sb("seg", [P, 4])
        spread = sb("spread", [P, 2, P])
        mask = sb("mask", [P, z.NI])
        tabf = sb("tabf", [P, 2, z.NI])

        ps_xT = [ctx.enter_context(nc.psum_tensor(f"ps_xT{i}", [P, 512], F32)) for i in range(2)]
        ps_kv = [ctx.enter_context(nc.psum_tensor(f"ps_kv{i}", [P, 512], F32)) for i in range(2)]
        ps_q = [ctx.enter_context(nc.psum_tensor(f"ps_q{i}", [P, 512], F32)) for i in range(2)]
        ps_n = ctx.enter_context(nc.psum_tensor("ps_n", [P, 512], F32))
        ps_m = ctx.enter_context(nc.psum_tensor("ps_m", [P, 512], F32))

        w_in = sem("w_in")
        x_in = sem("x_loaded")
        x_init = sem("x_init")
        feat_out = sem("feat_stored")
        kv_stored = sem("kv_stored")
        feat_rdy = sem("feat_ready")
        xT_ps = sem("xT_in_psum")
        xT_rdy = sem("xT_ready")
        kv_ps = sem("kv_in_psum")
        q_ps = sem("q_in_psum")
        kv_rdy = sem("kv_evacuated")
        q_rdy = sem("q_evacuated")
        dvec = sem("dve_step")
        passed = sem("dve_passed")
        idz = sem("ident_zeroed")
        iddone = sem("ident_done")
        cst = sem("pool_constants")
        trid = sem("tri_set")
        dst_in = sem("dst_loaded")
        src_in = sem("src_loaded")
        nxt_in = sem("next_loaded")
        padded = sem("index_tile_padded")
        tabs = sem("edge_tables_ready")
        tab_out = sem("edge_tables_stored")
        cnt_rdy = sem("indices_read")
        counted = sem("edges_counted")
        seg_ps = sem("segments_in_psum")
        item_rdy = sem("items_ready")
        base_ps = sem("bases_in_psum")
        mask_rdy = sem("mask_ready")
        w_ps = sem("w_in_psum")
        w_got = sem("w_read")
        sb_ps = sem("starts_in_psum")

        full = z.E // L
        rest = z.E - full * L
        full1 = (z.E - 1) // L
        rest1 = z.E - 1 - full1 * L
        xb = x[0:(z.NT - 1) * P, :].rearrange("(t p) f -> p t f", p=P)
        featb = feat_d.rearrange("(t p) f -> p t f", p=P)
        kvb = kv_d.rearrange("(t p) f -> t p f", p=P)
        block = ctx.enter_context(nc.Block())

        @block.sync
        def _(sp):
            for i, w in enumerate((Wk, Wv, Wq)):
                sp.dma_start(w_sb[:, :, i * F:(i + 1) * F], w.rearrange("(c p) n -> p c n", p=P)).then_inc(w_in, 16)
            sp.wait_ge(x_init, 1)
            if NB > 1:
                sp.dma_start(x_sb[:, :, :], xb[:, 0:TB, :]).then_inc(x_in, 32)
            if NB > 2:
                with sp.Fori(1, NB - 1) as b:
                    sp.wait_ge(feat_rdy, b * TB)
                    sp.dma_start(x_sb[:, :, :], xb[:, bass.ds(b * TB, TB), :]).then_inc(x_in, 32)
            sp.wait_ge(feat_rdy, (NB - 1) * TB)
            if TB > 1:
                sp.dma_start(x_sb[:, 0:TB - 1, :], xb[:, (NB - 1) * TB:NB * TB - 1, :]).then_inc(x_in, 16)
            sp.dma_start(x_sb[0:z.tail, TB - 1, :], x[(z.NT - 1) * P:z.N, :]).then_inc(x_in, 16)
            sp.wait_ge(tab_out, 16 * 5)
            sp.wait_ge(feat_out, 16 * NB)
            sp.wait_ge(kv_stored, 16 * z.NT)

        @block.gpsimd
        def _(pool):
            affine_identity(nc, pool, keep.ident[:, :], P, idz, iddone)
            nc.gpsimd.iota(keep.iota[:, :], [[1, P]], base=0, channel_multiplier=0,
                           allow_small_or_imprecise_dtypes=True).then_inc(cst, 1)
            nc.gpsimd.iota(keep.countdown[:, :], [[-1, HEADS]], base=HEADS, channel_multiplier=0,
                           allow_small_or_imprecise_dtypes=True).then_inc(cst, 1)
            nc.gpsimd.iota(thr[:, :], [[ITEM, z.E // ITEM + 2]], base=0, channel_multiplier=0,
                           allow_small_or_imprecise_dtypes=True).then_inc(cst, 1)
            nc.gpsimd.iota(item_no[:, :], [[1, z.NI]], base=0, channel_multiplier=0,
                           allow_small_or_imprecise_dtypes=True).then_inc(cst, 1)
            nc.gpsimd.iota(tile_no[:, :], [[1, z.NT + 1]], base=0, channel_multiplier=0,
                           allow_small_or_imprecise_dtypes=True).then_inc(cst, 1)
            nc.gpsimd.memset(tri[:, :], 1.0).then_inc(trid, 1)
            pool.wait_ge(trid, 1)
            nc.gpsimd.affine_select(out=tri[:, :], in_=tri[:, :], compare_op=ALU.is_ge, fill=0.0, base=0,
                                    pattern=[[1, P]], channel_multiplier=-1).then_inc(trid, 1)
            nc.gpsimd.memset(idx_i[:, :], z.PAD).then_inc(padded, 1)
            pool.wait_ge(padded, 1)
            pool.dma_start(idx_i[0:full, :], dst[0:full * L].rearrange("(p l) -> p l", l=L)).then_inc(dst_in, 16)
            pool.dma_start(idx_i[full:full + 1, 0:rest], dst[full * L:z.E].rearrange("(a l) -> a l", a=1)).then_inc(dst_in, 16)
            pool.wait_ge(cnt_rdy, 1)
            nc.gpsimd.memset(idx_i[:, :], z.PAD).then_inc(padded, 1)
            pool.wait_ge(padded, 2)
            pool.dma_start(idx_i[0:full1, :], dst[1:1 + full1 * L].rearrange("(p l) -> p l", l=L)).then_inc(nxt_in, 16)
            pool.dma_start(idx_i[full1:full1 + 1, 0:rest1],
                           dst[1 + full1 * L:z.E].rearrange("(a l) -> a l", a=1)).then_inc(nxt_in, 16)
            pool.wait_ge(cnt_rdy, 2)
            nc.gpsimd.memset(idx_i[:, :], 0).then_inc(padded, 1)
            pool.wait_ge(padded, 3)
            pool.dma_start(idx_i[0:full, :], src[0:full * L].rearrange("(p l) -> p l", l=L)).then_inc(src_in, 16)
            pool.dma_start(idx_i[full:full + 1, 0:rest], src[full * L:z.E].rearrange("(a l) -> a l", a=1)).then_inc(src_in, 16)
            pool.wait_ge(tabs, 1)
            for i, t in enumerate((src_f, dst_f, nxt_f)):
                pool.dma_start(etab_d[i].rearrange("(p l) -> p l", p=P), t[:, :]).then_inc(tab_out, 16)
            pool.wait_ge(tabs, 2)
            pool.dma_start(pen_d[1:1 + z.EP].rearrange("(p l) -> p l", p=P), dst_f[:, :]).then_inc(tab_out, 16)
            pool.dma_start(pen_d[0:1].rearrange("(a b) -> a b", a=1), below[0:1, 0:1]).then_inc(tab_out, 16)
            nc.gpsimd.memset(keep.acc[:, :], 0.0).then_inc(cst, 1)

        @block.scalar
        def _(act):
            def block_of(b):
                act.wait_ge(feat_rdy, (b + 1) * TB)
                act.dma_start(featb[:, bass.ds(b * TB, TB), :], feat[:, :, :]).then_inc(feat_out, 16)
                for j in range(TB):
                    t = b * TB + j
                    act.wait_ge(kv_ps, t + 1)
                    if j == 0 and not (isinstance(b, int) and b == 0):
                        act.wait_ge(kv_stored, 16 * TB * b)
                    nc.scalar.activation(kv_out[:, j, :], ps_kv[j % 2][:, :], ACT.Copy).then_inc(kv_rdy, 1)
                    act.wait_ge(q_ps, t + 1)
                    nc.scalar.activation(keep.q[:, bass.ds(t * F, F)], ps_q[j % 2][:, 0:F], ACT.Copy,
                                         scale=float(F) ** -0.5).then_inc(q_rdy, 1)
                    act.wait_ge(kv_rdy, t + 1)
                    act.dma_start(kvb[bass.ds(t, 1), :, :].rearrange("a p f -> (a p) f"), kv_out[:, j, :]).then_inc(kv_stored, 16)
            block_of(0)
            if NB > 1:
                with act.Fori(1, NB) as b:
                    block_of(b)

        @block.tensor
        def _(pe):
            pe.wait_ge(w_in, 48)
            pe.wait_ge(iddone, 1)

            def turn(b, j):
                t = b * TB + j
                pe.wait_ge(feat_rdy, t + 1)
                if j == 0:
                    if not isinstance(t, int) or t > 0:
                        pe.wait_ge(xT_rdy, t)
                elif j >= 2:
                    pe.wait_ge(xT_rdy, t - 1)
                for c in range(2):
                    mm = nc.tensor.transpose(ps_xT[j % 2][:, c * P:(c + 1) * P], feat[:, j, c * P:(c + 1) * P],
                                             keep.ident[:, :])
                mm.then_inc(xT_ps, 1)

            def products(b, j):
                t = b * TB + j
                s = j % 2
                pe.wait_ge(xT_rdy, t + 1)
                taken = t if j == 0 else t - 1 if j > 1 else 0
                if not isinstance(taken, int) or taken > 0:
                    pe.wait_ge(kv_rdy, taken)
                    pe.wait_ge(q_rdy, taken)
                for c in range(2):
                    mm = nc.tensor.matmul(ps_kv[s][:, :], featT[:, s, c, :], w_sb[:, c, 0:2 * F],
                                          start=(c == 0), stop=(c == 1))
                mm.then_inc(kv_ps, 1)
                for c in range(2):
                    mm = nc.tensor.matmul(ps_q[s][:, 0:F], featT[:, s, c, :], w_sb[:, c, 2 * F:3 * F],
                                          start=(c == 0), stop=(c == 1))
                mm.then_inc(q_ps, 1)

            turn(0, 0)

            def block_of(b):
                for j in range(TB):
                    turn(b + (j + 1) // TB, (j + 1) % TB)
                    products(b, j)
            block_of(0)
            if NB > 2:
                with pe.Fori(1, NB - 1) as b:
                    block_of(b)
            for j in range(TB):
                if j + 1 < TB:
                    turn(NB - 1, j + 1)
                products(NB - 1, j)
            pe.wait_ge(counted, 1)
            nc.tensor.matmul(ps_n[0:z.NT, 0:1], below[:, 0:z.NT], keep.ones[:, 0:1], start=True, stop=True)
            nc.tensor.matmul(ps_n[0:z.NT, 1:2], below[:, 1:z.NT + 1], keep.ones[:, 0:1], start=True,
                             stop=True).then_inc(seg_ps, 1)
            pe.wait_ge(item_rdy, 1)
            pe.wait_ge(trid, 2)
            nc.tensor.matmul(ps_n[0:z.NT, 2:3], tri[0:z.NT, 0:z.NT], seg[0:z.NT, 3:4], start=True,
                             stop=True).then_inc(base_ps, 1)
            pe.wait_ge(mask_rdy, 1)
            nc.tensor.matmul(ps_m[:, 0:z.NI], keep.ones[0:z.NT, :], mask[0:z.NT, :], start=True, stop=True).then_inc(w_ps, 1)
            nc.tensor.matmul(ps_n[:, 0:z.NI], spread[0:z.NT, 0, :], mask[0:z.NT, :], start=True, stop=True).then_inc(sb_ps, 1)
            pe.wait_ge(w_got, 1)
            nc.tensor.matmul(ps_m[:, 0:z.NI], spread[0:z.NT, 1, :], mask[0:z.NT, :], start=True, stop=True).then_inc(sb_ps, 1)

        @block.vector
        def _(dve):
            step = Chain(dve, dvec)
            nc.vector.memset(x_sb[:, :, :], 0.0).then_inc(x_init, 1)
            step(nc.vector.memset(keep.ones[:, :], 1.0))

            def stats_of(tiles):
                for j in tiles:
                    last = nc.vector.bn_stats(stats[:, j, :], x_sb[:, j, :])
                return last

            def moments():
                for j in range(TB):
                    last = nc.vector.bn_aggr(mv[:, j, :], stats[:, j, :])
                step(last)
                step(nc.vector.tensor_scalar(var[:, :], mv[:, :, 1], EPS, None, ALU.add))

            def feats(b, tiles):
                if not isinstance(b, int) or b > 0:
                    dve.wait_ge(feat_out, 16 * b)
                    dve.wait_ge(xT_ps, (b - 1) * TB + tiles[-1] + 1)
                for j in tiles:
                    nc.vector.tensor_scalar(feat[:, j, :], x_sb[:, j, :], mv[:, j, 0:1], rstd[:, j:j + 1],
                                            ALU.subtract, ALU.mult).then_inc(feat_rdy, 1)

            def take(b, j):
                t = b * TB + j
                dve.wait_ge(xT_ps, t + 1)
                if j == 0:
                    if not isinstance(t, int) or t > 0:
                        dve.wait_ge(q_ps, t)
                elif j >= 2:
                    dve.wait_ge(q_ps, t - 1)
                nc.vector.tensor_copy(featT[:, j % 2, :, :],
                                      ps_xT[j % 2][:, 0:2 * P].rearrange("p (c n) -> p c n", c=2)).then_inc(xT_rdy, 1)

            def count(b, j):
                w = b * TB + j + 1
                at = slice(w, w + 1) if isinstance(w, int) else bass.ds(w, 1)
                step(nc.vector.tensor_scalar(junk[:, :], dst_tile[:, :], tile_no[:, at], 0.0, ALU.is_lt, ALU.add,
                                             accum_out=below[:, at]))

            dve.wait_ge(dst_in, 32)
            step(nc.vector.tensor_scalar(src_f[:, :].bitcast(I32), idx_i[:, :], P.bit_length() - 1, None,
                                         ALU.logical_shift_right))
            step(nc.vector.tensor_copy(dst_tile[:, :], src_f[:, :].bitcast(I32)))
            nc.vector.tensor_copy(dst_f[:, :], idx_i[:, :]).then_inc(cnt_rdy, 1)
            dve.wait_ge(x_in, 32)
            step(stats_of(range(TB)), apart=passed)
            moments()
            rsqrt(nc, step, var[:, :], rstd[:, :], tmp[:, :])
            feats(0, range(TB))
            dve.wait_ge(cnt_rdy, 1)
            dve.wait_ge(nxt_in, 32)
            nc.vector.tensor_copy(nxt_f[:, :], idx_i[:, :]).then_inc(cnt_rdy, 1)
            take(0, 0)
            dve.wait_ge(cnt_rdy, 2)
            step(nc.vector.tensor_tensor(nxt_f[:, :], nxt_f[:, :], dst_f[:, :], ALU.not_equal))
            step(nc.vector.tensor_scalar(nxt_f[:, :], nxt_f[:, :], BIG, None, ALU.mult))
            dve.wait_ge(src_in, 32)
            nc.vector.tensor_copy(src_f[:, :], idx_i[:, :]).then_inc(tabs, 1)
            step(nc.vector.memset(below[:, :], 0.0))
            dve.wait_ge(cst, 5)
            pre = step.k

            def block_of(b, first_taken):
                if not first_taken:
                    take(b, 0)
                count(b, 0)
                dve.wait_ge(x_in, 32 * (b + 2))
                stats_of(range(TB // 2))
                take(b, 1)
                step(stats_of(range(TB // 2, TB)), apart=passed)
                count(b, 1)
                take(b, 2)
                moments()
                count(b, 2)
                take(b, 3)
                rsqrt(nc, step, var[:, :], rstd[:, :], tmp[:, :])
                take(b, 4)
                count(b, 3)
                feats(b + 1, range(2))
                take(b, 5)
                count(b, 4)
                feats(b + 1, range(2, 4))
                take(b, 6)
                feats(b + 1, range(4, TB))
                count(b, 5)
                count(b, 6)

            assert TB == 7
            block_of(0, True)
            per = step.k - pre
            if NB > 2:
                with dve.Fori(1, NB - 1) as b:
                    step.k, step.base = 0, pre + b * per
                    block_of(b, False)
            step.k, step.base = 0, pre + (NB - 1) * per
            dve.wait_ge(tab_out, 48)
            nc.vector.tensor_scalar(dst_f[:, :], nxt_f[:, :], -1.0, None, ALU.mult).then_inc(tabs, 1)
            for j in range(TB):
                take(NB - 1, j)
                count(NB - 1, j)
            dve.wait_ge(iddone, 1)
            dve.sem_inc(counted, 1)
            nt = z.NT
            dve.wait_ge(seg_ps, 1)
            step(nc.vector.tensor_copy(seg[0:nt, 0:2], ps_n[0:nt, 0:2]))
            step(nc.vector.tensor_tensor(seg[0:nt, 2:3], seg[0:nt, 1:2], seg[0:nt, 0:1], ALU.subtract))
            nc.vector.tensor_scalar(junk2[0:nt, :], thr[0:nt, :], seg[0:nt, 2:3], 0.0, ALU.is_lt, ALU.add,
                                    accum_out=seg[0:nt, 3:4]).then_inc(item_rdy, 1)
            dve.wait_ge(item_rdy, 1)
            for i in range(2):
                step(nc.vector.tensor_scalar(spread[0:nt, i, :], keep.ones[0:nt, :], seg[0:nt, 2 + i:3 + i], None, ALU.mult))
            dve.wait_ge(base_ps, 1)
            nc.vector.tensor_scalar(mask[0:nt, :], item_no[0:nt, :], ps_n[0:nt, 2:3], None, ALU.is_ge).then_inc(mask_rdy, 1)
            dve.wait_ge(w_ps, 1)
            nc.vector.tensor_scalar(tabf[:, 0, :], ps_m[:, 0:z.NI], float(nt - 1), None, ALU.min).then_inc(w_got, 1)
            dve.wait_ge(w_got, 1)
            step(nc.vector.tensor_copy(keep.w_i[:, :], tabf[:, 0, :]))
            step(nc.vector.tensor_scalar(keep.minus_first[:, :], tabf[:, 0, :], -float(P), None, ALU.mult))
            dve.wait_ge(sb_ps, 2)
            step(nc.vector.tensor_tensor(tabf[:, 1, :], item_no[:, :], ps_m[:, 0:z.NI], ALU.subtract))
            step(nc.vector.scalar_tensor_tensor(out=tabf[:, 1, :], in0=tabf[:, 1, :], scalar=float(ITEM),
                                                in1=ps_n[:, 0:z.NI], op0=ALU.mult, op1=ALU.add))
            step(nc.vector.tensor_scalar(keep.e_i[:, :], tabf[:, 1, :], float(z.E), None, ALU.min))
            step(nc.vector.tensor_tensor(tabf[:, 0, 1:z.NI], keep.minus_first[:, 1:z.NI], keep.minus_first[:, 0:z.NI - 1], ALU.not_equal))
            step(nc.vector.memset(keep.reset[:, 0:1], -2.0 * BIG))
            step(nc.vector.tensor_scalar(keep.reset[:, 1:z.NI], tabf[:, 0, 1:z.NI], -2.0 * BIG, None, ALU.mult))
            step(nc.vector.tensor_scalar(keep.lastcol[:, :], keep.ident[:, P - 1:P], BIG, None, ALU.mult))
            step(nc.vector.tensor_scalar(keep.notlast[:, :], keep.ident[:, P - 1:P], -1.0, 1.0, ALU.mult, ALU.add))
            dve.wait_ge(cst, 6)


def edge_phase(nc, z, kv_d, etab_d, pen_d, keep):
    NI, R = z.NI, RING
    with ExitStack() as ctx:
        def sb(name, shape, dt=F32):
            return ctx.enter_context(nc.sbuf_tensor(name, shape, dt))

        def sem(name):
            return ctx.enter_context(nc.semaphore(name))

        rows = sb("idx_rows", [3 * SUB, R, P])
        pen = sb("pen", [SUB * HEADS, R, P])
        idx = sb("idx", [P, R, SUB], I32)
        rel = sb("rel", [P, R, SUB])
        sel = sb("sel", [P, R, SUB, HEADS + 1])
        kv = sb("kv", [P, R, SUB, 2 * F])
        sq = sb("sq", [P, SUB, P], BF16)
        oh32 = sb("oh32", [P, R, SUB, P])
        ohT = sb("ohT", [P, QR, SUB, P], F32R)
        q_hi = sb("q_hi", [P, QR, F], F32R)
        q_lo = sb("q_lo", [P, QR, F], F32R)
        prod = sb("prod", [P, SUB, F])
        score = sb("score", [P, R, SUB * HEADS])
        run = sb("run", [SUB * HEADS, R, P])
        absent = sb("absent", [P, SUB])
        cand = sb("cand", [P, SUB, HEADS])
        top = sb("top", [P, HEADS])
        mnew = sb("mnew", [P, R, HEADS])
        mdif = sb("mdif", [P, R, HEADS])
        alpha = sb("alpha", [P, R, HEADS])
        arg = sb("arg", [P, R, SUB * HEADS])
        pv = sb("pv", [P, 2, SUB, FA])

        def bank(name, dt=F32):
            return ctx.enter_context(nc.psum_tensor(name, [P, 2048 // (4 if dt == F32 else 2)], dt))

        ps_q = ctx.enter_context(nc.psum_tensor("ps_qx", [P, SUB * F], F32))
        ps_oh = bank("ps_oh")
        ps_agg = [bank("ps_agg0"), bank("ps_agg1")]
        ps_idx = bank("ps_idx")
        ps_s = bank("ps_scores")
        ps_m = bank("ps_maxima")

        rows_in = [sem(f"rows_loaded{i}") for i in range(R)]
        kv_in = [sem(f"kv_loaded{i}") for i in range(R)]
        idx_ps = sem("idx_in_psum")
        idx_rdy = sem("idx_ready")
        rel_rdy = sem("rel_ready")
        oh_rdy = sem("onehot_ready")
        sq_rdy = sem("squares_ready")
        ohT_ps = sem("onehotT_in_psum")
        ohT_rdy = sem("onehotT_ready")
        q_ps = sem("q_rows_in_psum")
        prod_rdy = sem("prod_ready")
        dots_rdy = sem("dots_ready")
        eT_ps = sem("scoresT_in_psum")
        run_rdy = sem("running_max_ready")
        back_ps = sem("running_max_in_psum")
        sel_rdy = sem("last_selected")
        msel_ps = sem("tile_max_in_psum")
        m_step = sem("max_step")
        first_max = sem("first_max_set")
        m_rdy = sem("new_max_ready")
        me_ps = sem("edge_max_in_psum")
        arg_rdy = sem("exponent_ready")
        p_rdy = sem("p_ready")
        al_rdy = sem("alpha_ready")
        pv_rdy = sem("pv_ready")
        pv_last = sem("pv_last_tile_ready")
        hi_rdy = sem("q_high_ready")
        lo_rdy = sem("q_low_ready")
        act_passed = sem("act_passed")
        agg_ps = sem("sums_in_psum")
        acc_half = sem("acc_scaled")
        acc_rdy = sem("acc_ready")
        pe_passed = sem("pe_passed")
        pool_passed = sem("pool_passed")

        block = ctx.enter_context(nc.Block())

        def pipeline(eng, step):
            last = NI // R - 1
            for base in (-R, 0, R):
                for k in range(R):
                    step(base, k)
            with eng.Fori(2, last) as turn:
                for k in range(R):
                    step(turn * R, k)
            for base in range(last * R, NI + LAG, R):
                for k in range(R):
                    step(base, k)

        def item(base, k, lag):
            j = k + lag
            if isinstance(base, int):
                n = base + j
                if n < 0 or n >= NI:
                    return None
                return n, j % R
            return base + j, j % R

        def wait(eng, s, value):
            if not (isinstance(value, int) and value <= 0):
                eng.wait_ge(s, value)

        def wait_apart(eng, passed, *waits):
            for sem_, v in waits:
                wait(eng, sem_, v)
            eng.sem_inc(passed, 1)

        def wait_slot(eng, s, n, slot, per):
            if isinstance(n, int):
                eng.wait_ge(s, per * ((n - slot) // R + 1))
            else:
                eng.wait_ge(s, (n - slot + R) // R * per)

        @block.sync
        def _(sp):
            def load(base, k):
                it = item(base, k, 5)
                if it is None:
                    return
                n, s = it
                wait(sp, idx_ps, n - R + 1)
                wait(sp, run_rdy, n - R + 1)
                e = sp.value_load(keep.e_i[0:1, bass.ds(n, 1)], min_val=0, max_val=z.E)
                for i in range(3):
                    sp.dma_start(rows[i * SUB:(i + 1) * SUB, s, :],
                                 etab_d[i, bass.ds(e, ITEM)].rearrange("(g p) -> g p", p=P)).then_inc(rows_in[s], 16)
                for g in range(SUB):
                    sp.dma_start(pen[g * HEADS:(g + 1) * HEADS, s, :],
                                 pen_d[bass.ds(e + g * P, P)].rearrange("(a p) -> a p", a=1).to_broadcast([HEADS, P]),
                                 ).then_inc(rows_in[s], 16)
            pipeline(sp, load)

        LOADS = 16 * (3 + SUB)

        @block.gpsimd
        def _(pool):
            def gather(base, k):
                it = item(base, k, 3)
                if it is None:
                    return
                n, s = it
                wait_apart(pool, pool_passed, (idx_rdy, n + 1), (pv_rdy, n - R + 1), (pv_last, n - R + 1))
                for g in range(SUB):
                    pool.indirect_dma_start(
                        out=kv[:, s, g, :], out_offset=None, in_=kv_d,
                        in_offset=bass.IndirectOffsetOnAxis(ap=idx[:, s, g:g + 1], axis=0),
                    ).then_inc(kv_in[s], 16)

            def q_rest(base, k):
                it = item(base, k, 2)
                if it is None:
                    return
                n, s = it
                wait_apart(pool, pool_passed, (hi_rdy, n + 1), (q_ps, n - QR + 1))
                w = pool.value_load(keep.w_i[0:1, bass.ds(n, 1)], min_val=0, max_val=z.NT - 1)
                nc.gpsimd.tensor_tensor(q_lo[:, s % QR, :], keep.q[:, bass.ds(w * F, F)], q_hi[:, s % QR, :],
                                        ALU.subtract).then_inc(lo_rdy, 1)

            def go(base, k):
                gather(base, k)
                q_rest(base, k)
            pipeline(pool, go)

        @block.scalar
        def _(act):
            def go(base, k):
                it = item(base, k, 3)
                if it is not None:
                    n, s = it
                    act.wait_ge(idx_ps, n + 1)
                    wait(act, pv_rdy, n - R + 1)
                    nc.scalar.activation(idx[:, s, :], ps_idx[:, 0:SUB], ACT.Copy).then_inc(idx_rdy, 1)
                    nc.scalar.activation(rel[:, s, :], ps_idx[:, SUB:2 * SUB], ACT.Identity,
                                         bias=keep.minus_first[:, bass.ds(n, 1)])
                    wait(act, msel_ps, n - R + 1)
                    nc.scalar.activation(sel[:, s, :, HEADS], ps_idx[:, 2 * SUB:3 * SUB], ACT.Identity,
                                         bias=keep.lastcol[:, 0:1], scale=keep.notlast[:, 0:1]).then_inc(rel_rdy, 1)
                it = item(base, k, 1)
                if it is not None:
                    n, s = it
                    act.wait_ge(ohT_ps, n + 1)
                    wait(act, me_ps, n - QR + 1)
                    nc.scalar.activation(ohT[:, s % QR, :, :], ps_oh[:, :].rearrange("p (g n) -> p g n", g=SUB),
                                         ACT.Copy).then_inc(ohT_rdy, 1)
                it = item(base, k, 2)
                if it is not None:
                    n, s = it
                    wait_apart(act, act_passed, (q_ps, n - QR + 1))
                    w = act.value_load(keep.w_i[0:1, bass.ds(n, 1)], min_val=0, max_val=z.NT - 1)
                    nc.scalar.activation(q_hi[:, s % QR, :], keep.q[:, bass.ds(w * F, F)], ACT.Copy).then_inc(hi_rdy, 1)
                it = item(base, k, -2)
                if it is not None:
                    n, s = it
                    act.wait_ge(arg_rdy, n + 1)
                    wait(act, agg_ps, n - 1)
                    nc.scalar.activation(pv[:, s % 2, :, :].rearrange("p g (h c) -> p (g h) c", c=HC)[:, :, DH],
                                         arg[:, s, :], ACT.Exp).then_inc(p_rdy, 1)
                    wait(act, acc_half, n - 1)
                    nc.scalar.activation(alpha[:, s, :], mdif[:, s, :], ACT.Exp).then_inc(al_rdy, 1)
                it = item(base, k, -2)
                if it is not None:
                    n, s = it
                    g = SUB - 1
                    act.wait_ge(p_rdy, n + 1)
                    wait_slot(act, kv_in[s], n, s, 16 * SUB)
                    for h in range(HEADS):
                        last = nc.scalar.activation(pv[:, s % 2, g, h * HC:h * HC + DH],
                                                    kv[:, s, g, F + h * DH:F + (h + 1) * DH], ACT.Copy,
                                                    scale=pv[:, s % 2, g, h * HC + DH:(h + 1) * HC])
                    last.then_inc(pv_last, 1)
                it = item(base, k, 3)
                if it is not None:
                    n, s = it
                    act.wait_ge(rel_rdy, n + 1)
                    wait(act, oh_rdy, n)
                    for g in range(SUB):
                        last = nc.scalar.activation(sq[:, g, :], keep.iota[:, :], ACT.Square, bias=rel[:, s, g:g + 1], scale=-1.0)
                    last.then_inc(sq_rdy, 1)
                    act.wait_ge(sq_rdy, n + 1)
                    wait(act, agg_ps, n - R + 1)
                    nc.scalar.activation(oh32[:, s, :, :], sq[:, :, :], ACT.Relu, bias=keep.ones[:, 0:1],
                                         scale=-2.0).then_inc(oh_rdy, 1)
            pipeline(act, go)

        @block.tensor
        def _(pe):
            def sums(it, tiles):
                n, s = it
                if tiles[0] == 0:
                    pe.wait_ge(pv_rdy, n + 1)
                    wait(pe, acc_rdy, n - 1)
                if tiles[-1] == SUB - 1:
                    pe.wait_ge(pv_last, n + 1)
                for g in tiles:
                    mm = nc.tensor.matmul(ps_agg[s % 2][:, 0:FA], oh32[:, s, g, :], pv[:, s % 2, g, :],
                                          start=(g == 0), stop=(g == SUB - 1))
                if tiles[-1] == SUB - 1:
                    mm.then_inc(agg_ps, 1)

            def q_rows(it):
                n, s = it
                pe.wait_ge(ohT_rdy, n + 1)
                pe.wait_ge(lo_rdy, n + 1)
                wait(pe, prod_rdy, n)
                for g in range(SUB):
                    for part in range(2):
                        q = (q_hi, q_lo)[part][:, s % QR, :]
                        mm = nc.tensor.matmul(ps_q[:, g * F:(g + 1) * F], ohT[:, s % QR, g, :], q,
                                              start=(part == 0), stop=(part == 1))
                mm.then_inc(q_ps, 1)

            def go(base, k):
                it = item(base, k, -1)
                if it is not None:
                    n, s = it
                    wait_apart(pe, pe_passed, (run_rdy, n + 1))
                    nc.tensor.transpose(ps_s[:, 128:128 + SUB * HEADS], run[:, s, :],
                                        keep.ident[0:SUB * HEADS, 0:SUB * HEADS]).then_inc(back_ps, 1)
                agg_it, q_it = item(base, k, -3), item(base, k, 1)
                if agg_it is not None:
                    sums(agg_it, range(SUB // 2))
                it = item(base, k, -1)
                if it is not None:
                    n, s = it
                    pe.wait_ge(sel_rdy, n + 1)
                    wait(pe, arg_rdy, n)
                    for g in range(SUB):
                        mm = nc.tensor.matmul(ps_m[:, 9 * g:9 * g + 9], oh32[:, s, g, :], sel[:, s, g, :],
                                              start=True, stop=True)
                    mm.then_inc(msel_ps, 1)
                if agg_it is not None:
                    sums(agg_it, range(SUB // 2, SUB))
                it = item(base, k, 0)
                if it is not None:
                    n, s = it
                    pe.wait_ge(dots_rdy, n + 1)
                    wait(pe, sel_rdy, n)
                    nc.tensor.transpose(ps_s[0:SUB * HEADS, 0:P], score[:, s, :], keep.ident[:, :]).then_inc(eT_ps, 1)
                if q_it is not None:
                    q_rows(q_it)
                it = item(base, k, -1)
                if it is not None:
                    n, s = it
                    pe.wait_ge(m_rdy, n + 1)
                    for g in range(SUB):
                        mm = nc.tensor.matmul(ps_m[:, 64 + 8 * g:72 + 8 * g], ohT[:, s % QR, g, :].bitcast(F32), mnew[:, s, :],
                                              start=True, stop=True)
                    mm.then_inc(me_ps, 1)
                it = item(base, k, 2)
                if it is not None:
                    n, s = it
                    pe.wait_ge(oh_rdy, n + 1)
                    wait(pe, ohT_rdy, n)
                    for g in range(SUB):
                        mm = nc.tensor.transpose(ps_oh[:, g * P:(g + 1) * P], oh32[:, s, g, :], keep.ident[:, :])
                    mm.then_inc(ohT_ps, 1)
                it = item(base, k, 4)
                if it is not None:
                    n, s = it
                    wait_slot(pe, rows_in[s], n, s, LOADS)
                    wait_apart(pe, pe_passed, (rel_rdy, n))
                    nc.tensor.transpose(ps_idx[:, 0:3 * SUB], rows[:, s, :], keep.ident[0:3 * SUB, 0:3 * SUB]).then_inc(idx_ps, 1)
            pipeline(pe, go)

        @block.vector
        def _(dve):
            def p_times_v(s, g):
                out = pv[:, s % 2, g, :].rearrange("p (h c) -> p h c", c=HC)
                return nc.vector.tensor_tensor(out[:, :, 0:DH], kv[:, s, g, F:2 * F].rearrange("p (h d) -> p h d", d=DH),
                                               out[:, :, DH:HC].to_broadcast([P, HEADS, DH]), ALU.mult)

            def go(base, k):
                it = item(base, k, -1)
                if it is not None:
                    n, s = it
                    dve.wait_ge(eT_ps, n + 1)
                    wait_slot(dve, rows_in[s], n, s, LOADS)
                    wait(dve, back_ps, n - R + 1)
                    nc.vector.tensor_tensor_scan(run[:, s, :], pen[:, s, :], ps_s[0:SUB * HEADS, 0:P], -BIG,
                                                 ALU.add, ALU.max).then_inc(run_rdy, 1)
                it = item(base, k, 0)
                if it is not None:
                    n, s = it
                    wait_slot(dve, kv_in[s], n, s, 16 * SUB)
                    dve.wait_ge(q_ps, n + 1)
                    wait(dve, dots_rdy, n)
                    nc.vector.tensor_tensor(prod[:, :, :], kv[:, s, :, 0:F],
                                            ps_q[:, :].rearrange("p (g f) -> p g f", g=SUB), ALU.mult).then_inc(prod_rdy, 1)
                it = item(base, k, -2)
                if it is not None:
                    n, s = it
                    dve.wait_ge(me_ps, n + 1)
                    nc.vector.tensor_tensor(arg[:, s, :], score[:, s, :], ps_m[:, 64:64 + SUB * HEADS],
                                            ALU.subtract).then_inc(arg_rdy, 1)
                it = item(base, k, -1)
                if it is not None:
                    n, s = it
                    dve.wait_ge(back_ps, n + 1)
                    dve.wait_ge(rel_rdy, n + 1)
                    nc.vector.scalar_tensor_tensor(
                        out=sel[:, s, :, 0:HEADS], in0=sel[:, s, :, HEADS:HEADS + 1].to_broadcast([P, SUB, HEADS]),
                        scalar=1.0 / BIG, in1=ps_s[:, 128:128 + SUB * HEADS].rearrange("p (g h) -> p g h", h=HEADS),
                        op0=ALU.mult, op1=ALU.mult).then_inc(sel_rdy, 1)
                it = item(base, k, 0)
                if it is not None:
                    n, s = it
                    dve.wait_ge(prod_rdy, n + 1)
                    wait(dve, arg_rdy, n - R + 1)
                    nc.vector.tensor_reduce(score[:, s, :], prod[:, :, :].rearrange("p g (h d) -> p (g h) d", d=DH),
                                            AX.X, ALU.add).then_inc(dots_rdy, 1)
                it = item(base, k, -3)
                if it is not None:
                    w_acc = dve.value_load(keep.w_i[0:1, bass.ds(it[0], 1)], min_val=0, max_val=z.NT - 1)
                m, v, a = item(base, k, -1), item(base, k, -2), item(base, k, -3)
                if m is not None:
                    dve.wait_ge(msel_ps, m[0] + 1)
                    tile_max = ps_m[:, 0:9 * SUB].rearrange("p (g h) -> p g h", h=HEADS + 1)
                    nc.vector.tensor_scalar(absent[:, :], tile_max[:, :, HEADS], -BIG, None, ALU.add).then_inc(m_step, 1)
                if v is not None:
                    dve.wait_ge(p_rdy, v[0] + 1)
                    wait(dve, agg_ps, v[0] - 1)
                    p_times_v(v[1], 0)
                if m is not None:
                    dve.wait_ge(m_step, 4 * m[0] + 1)
                    nc.vector.tensor_tensor(cand[:, :, :], tile_max[:, :, 0:HEADS],
                                            absent[:, :].rearrange("p (g a) -> p g a", a=1).to_broadcast([P, SUB, HEADS]),
                                            ALU.add).then_inc(m_step, 1)
                if v is not None:
                    p_times_v(v[1], 1)
                if m is not None:
                    dve.wait_ge(m_step, 4 * m[0] + 2)
                    nc.vector.tensor_reduce(top[:, :], cand[:, :, :].rearrange("p g h -> p h g"), AX.X, ALU.max).then_inc(m_step, 1)
                if v is not None:
                    p_times_v(v[1], 2).then_inc(pv_rdy, 1)
                if m is not None:
                    n, s = m
                    before = mnew[:, (s - 1) % R, :]
                    reset = keep.reset[:, bass.ds(n, 1)]
                    dve.wait_ge(m_step, 4 * n + 3)
                    wait(dve, m_rdy, n)
                    wait(dve, me_ps, n - R + 1)
                    nc.vector.scalar_tensor_tensor(out=mnew[:, s, :], in0=before, scalar=reset, in1=top[:, :],
                                                   op0=ALU.add, op1=ALU.max).then_inc(m_rdy, 1)
                if a is not None:
                    n, s = a
                    acc = keep.acc[:, bass.ds(w_acc * FA, FA)]
                    dve.wait_ge(al_rdy, n + 1)
                    wait(dve, acc_rdy, n)
                    nc.vector.tensor_tensor(acc.rearrange("p (h c) -> p h c", c=HC), acc.rearrange("p (h c) -> p h c", c=HC),
                                            alpha[:, s, :].rearrange("p (h a) -> p h a", a=1).to_broadcast([P, HEADS, HC]),
                                            ALU.mult).then_inc(acc_half, 1)
                if m is not None:
                    n, s = m
                    dve.wait_ge(m_rdy, n + 1)
                    wait(dve, al_rdy, n - R + 1)
                    nc.vector.scalar_tensor_tensor(out=mdif[:, s, :], in0=before, scalar=reset, in1=mnew[:, s, :],
                                                   op0=ALU.add, op1=ALU.subtract).then_inc(m_step, 1)
                if a is not None:
                    n, s = a
                    dve.wait_ge(acc_half, n + 1)
                    dve.wait_ge(agg_ps, n + 1)
                    nc.vector.tensor_tensor(acc, acc, ps_agg[s % 2][:, 0:FA], ALU.add).then_inc(acc_rdy, 1)
            nc.vector.memset(mnew[:, R - 1, :], 0.0).then_inc(first_max, 1)
            dve.wait_ge(first_max, 1)
            pipeline(dve, go)


class Turns:

    def __init__(self, first, sizes):
        self.first, self.sizes = first, sizes

    def before(self, b):
        if isinstance(b, int):
            return sum(self.sizes(i) for i in range(self.first, b))
        return b * self.sizes(0) + sum(self.sizes(i) for i in range(self.first, 0))


def ffn_phase(nc, z, w, x, feat_d, out, keep):
    TB, NB, X, H1 = z.TB, z.NB, z.X, z.H1
    M1 = H1 // P
    KC = F // P
    TOK = TB * P
    CH = -(-TOK // 512)
    CW = TOK // CH
    G = -(-TB // 2)
    G += G % 2
    assert NB >= 2 and X == HEADS and TOK % CH == 0 and (M1 * CH) % 4 == 0 and (X * KC * CH) % 4 == 0
    with ExitStack() as ctx:
        def sb(name, shape, dt=F32):
            return ctx.enter_context(nc.sbuf_tensor("f_" + name, shape, dt))

        def sem(name):
            return ctx.enter_context(nc.semaphore("f_" + name))

        def bank(name):
            return ctx.enter_context(nc.psum_tensor(name, [P, 512], F32))

        w1 = sb("w1", [P, KC, H1])
        w2 = sb("w2", [P, M1, F])
        ew1 = sb("ew1", [P, X, KC, F])
        ew2 = sb("ew2", [P, X, KC, F])
        eb2 = sb("eb2", [X, F])
        ln_g = sb("ln_g_rows", [P, F])
        ln_b = sb("ln_b_rows", [P, F])
        b2 = sb("b2_rows", [P, F])
        nrows = 2 * M1 + X * KC
        bias_rows = sb("bias_rows", [nrows, P])
        bias = sb("bias", [P, nrows])
        rt_rows = sb("router_rows", [X, F])
        router = sb("routerT", [P, KC, X])
        feat = sb("feat_in", [P, TB, F])
        r1 = sb("r1", [P, TB, F])
        r1T = sb("r1T", [P, KC, TOK])
        hT = sb("hiddenT", [P, M1, TOK])
        bend = sb("bend", [P, 2, CW])
        side = sb("side", [P, M1])
        rise = sb("rise", [P, M1])
        rise_b = sb("rise_b1", [P, M1])
        slope = sb("side_alpha", [P, M1])
        slope_b = sb("side_alpha_b1", [P, M1])
        h2 = sb("h2", [P, TB, F])
        xo = sb("x_out", [P, TB, F])
        t = sb("tokens", [P, TB, F])
        tT = sb("tokensT", [P, KC, TOK])
        den = sb("den", [P, TB * HEADS])
        stats = sb("stats", [P, TB, 6])
        mv = sb("mv", [P, TB, 2])
        var = sb("var", [P, TB])
        rstd = sb("rstd", [P, TB])
        tmp = sb("tmp", [P, TB])
        prob = sb("prob", [P, TB, X])
        pick = sb("pick", [P, 3, TB, X])
        best = sb("best", [P, 2, TB])
        comb = sb("comb", [P, TB, X])
        combT = sb("combT", [X, TOK])

        ps_h = [bank(f"ps_h{i}") for i in range(4)]
        ps_y = [bank(f"ps_y{i}") for i in range(2)]
        ps_t = [bank(f"ps_t{i}") for i in range(2)]

        small_in = sem("small_weights_loaded")
        w1_in = sem("W1_loaded")
        w2_in = sem("W2_loaded")
        w2_rdy = sem("W2_with_side")
        ew_in = sem("expert_weights_loaded")
        feat_in = sem("feat_loaded")
        x_in = sem("x_loaded")
        out_st = sem("out_stored")
        dvec = sem("dve_step")
        passed = sem("dve_passed")
        setup_ps = sem("setup_in_psum")
        setup_rdy = sem("setup_ready")
        r1_rdy = sem("r1_ready")
        t_rdy = sem("tokens_ready")
        tr_ps = sem("transposed_in_psum")
        tr_rdy = sem("transposed_ready")
        h_ps = sem("hidden_in_psum")
        h_rdy = sem("hidden_ready")
        prelu_rdy = sem("prelu_ready")
        y_ps = sem("rows_in_psum")
        y_rdy = sem("rows_taken")
        rows_done = sem("block_rows_done")
        lg_rdy = sem("logits_less_max")
        pe_rdy = sem("exp_ready")
        zero_rdy = sem("x_zeroed")

        spots = [[] for _ in range(X)]
        for j in range(TB):
            spots[min(X - 1, X - 3 + j // 3)].append(j)

        has_ffn = lambda b: isinstance(b, int) and -1 <= b <= NB - 2 or not isinstance(b, int)
        has_moe = lambda b: not isinstance(b, int) or 0 <= b
        has_pre = lambda b: not isinstance(b, int) or b <= NB - 3
        y_turn = Turns(-2, lambda b: G * (has_ffn(b) + (1 + X) * has_moe(b)))
        h_turn = Turns(-2, lambda b: CH * (M1 * has_ffn(b) + X * KC * has_moe(b)))
        t_turn = Turns(-2, lambda b: (TB + 1 + 2) * has_moe(b) + TB * has_pre(b))

        def iterations(eng, body, peeled=0):
            for b in range(-2, min(peeled, NB - 2)):
                body(b)
            if NB - 2 > peeled:
                with eng.Fori(peeled, NB - 2) as b:
                    body(b)
            body(NB - 2)
            body(NB - 1)

        def wait(eng, s, value):
            if not (isinstance(value, int) and value <= 0):
                eng.wait_ge(s, value)

        xb = x[0:(z.NT - 1) * P, :].rearrange("(t p) f -> p t f", p=P)
        ob = out[0:(z.NT - 1) * P, :].rearrange("(t p) f -> p t f", p=P)
        featb = feat_d.rearrange("(t p) f -> p t f", p=P)
        block = ctx.enter_context(nc.Block())

        def groups():
            tiles = [list(range(i, min(i + 2, TB))) for i in range(0, TB, 2)]
            while len(tiles) < G:
                big = max(tiles, key=len)
                at = tiles.index(big)
                tiles[at:at + 1] = [big[:1], big[1:]] if len(big) > 1 else [big, []]
            return tiles

        GROUPS = groups()
        assert G == 4
        PLAN = [[(True, g) for g in range(G)] for _ in range(X)]
        PLAN[0] = [(True, 0), (True, 1), (True, 2), (False, 0), (True, 3), (False, 1)]
        PLAN[1] = [(True, 0), (False, 2), (True, 1), (False, 3), (True, 2), (True, 3)]

        def uses(b, e):
            return (G if has_ffn(b) else 0) + sum(len(PLAN[i]) for i in range(e))

        @block.sync
        def _(sp):
            small = [(bias_rows[0:M1, :], w.b1.rearrange("(m p) -> m p", p=P)),
                     (bias_rows[M1:2 * M1, :], w.alpha.rearrange("(m p) -> m p", p=P)),
                     (bias_rows[2 * M1:nrows, :], w.eb1.rearrange("e (c p) -> (e c) p", p=P)),
                     (rt_rows[:, :], w.router),
                     (eb2[:, :], w.eb2)]
            small += [(o[:, :], v.rearrange("(a n) -> a n", a=1).to_broadcast([P, F]))
                      for o, v in ((ln_g, w.ln_g), (ln_b, w.ln_b), (b2, w.b2))]
            experts = []
            for e in range(X):
                experts += [(ew1[:, e, :, :], w.ew1[e].rearrange("(c p) n -> p c n", p=P)),
                            (ew2[:, e, :, :], w.ew2[e].rearrange("(c p) n -> p c n", p=P))]
            sp.dma_start(feat[:, :, :], featb[:, 0:TB, :]).then_inc(feat_in, 16)
            for o, v in small:
                sp.dma_start(o, v).then_inc(small_in, 16)
            sp.dma_start(w1[:, :, :], w.W1.rearrange("(c p) n -> p c n", p=P)).then_inc(w1_in, 16)
            sp.dma_start(w2[:, :, :], w.W2.rearrange("(c p) n -> p c n", p=P)).then_inc(w2_in, 16)
            for o, v in experts:
                sp.dma_start(o, v).then_inc(ew_in, 16)

            def body(b):
                if has_pre(b) and not (isinstance(b, int) and b == -2):
                    sp.wait_ge(r1_rdy, b + 2)
                    sp.dma_start(feat[:, :, :], featb[:, bass.ds((b + 2) * TB, TB), :]).then_inc(feat_in, 16)
                if has_moe(b):
                    wait(sp, out_st, 16 * b)
                    if isinstance(b, int) and b == 0:
                        sp.wait_ge(zero_rdy, 1)
                    if isinstance(b, int) and b == NB - 1:
                        sp.dma_start(xo[0:z.tail, TB - 1, :], x[(z.NT - 1) * P:z.N, :]).then_inc(x_in, 16)
                        sp.dma_start(xo[:, 0:TB - 1, :], xb[:, b * TB:b * TB + TB - 1, :]).then_inc(x_in, 16)
                    else:
                        if not isinstance(b, int):
                            sp.wait_ge(zero_rdy, 1)
                        sp.dma_start(xo[:, :, :], xb[:, bass.ds(b * TB, TB), :]).then_inc(x_in, 32)
                    sp.wait_ge(rows_done, b + 1)
                    if isinstance(b, int) and b == NB - 1:
                        sp.dma_start(ob[:, b * TB:b * TB + TB - 1, :], xo[:, 0:TB - 1, :]).then_inc(out_st, 16)
                        sp.dma_start(out[(z.NT - 1) * P:z.N, :], xo[0:z.tail, TB - 1, :]).then_inc(out_st, 16)
                    else:
                        sp.dma_start(ob[:, bass.ds(b * TB, TB), :], xo[:, :, :]).then_inc(out_st, 16)
            iterations(sp, body, peeled=1)
            sp.wait_ge(out_st, 16 * (NB + 1))

        @block.tensor
        def _(pe):
            pe.wait_ge(small_in, 16 * 8)
            nc.tensor.transpose(ps_t[0][:, 0:nrows], bias_rows[:, :], keep.ident[0:nrows, 0:nrows])
            for c in range(KC):
                mm = nc.tensor.transpose(ps_t[0][:, 64 + c * X:64 + (c + 1) * X], rt_rows[:, c * P:(c + 1) * P],
                                         keep.ident[0:X, 0:X])
            mm.then_inc(setup_ps, 1)
            pe.wait_ge(setup_rdy, 1)

            def ffn(b):
                u = h_turn.before(b)
                pe.wait_ge(tr_rdy, t_turn.before(b))
                if isinstance(b, int) and b == -1:
                    pe.wait_ge(w1_in, 16)
                i = 0
                for m in range(M1):
                    for c in range(CH):
                        wait(pe, h_rdy, u + i - 3)
                        for k in range(KC):
                            mm = nc.tensor.matmul(ps_h[i % 4][:, 0:CW], w1[:, k, m * P:(m + 1) * P],
                                                  r1T[:, k, c * CW:(c + 1) * CW], start=(k == 0), stop=(k == KC - 1))
                        mm.then_inc(h_ps, 1)
                        i += 1

                def bent(m):
                    pe.wait_ge(prelu_rdy, M1 * CH * (b + 1) + CH * (m + 1))

                def tokens_turned(g):
                    if has_moe(b):
                        if g == 0:
                            pe.wait_ge(t_rdy, b + 1)
                        for j in GROUPS[g]:
                            turn_rows(t, j, j % 2, t_turn.before(b) + j, j == 0)
                if isinstance(b, int) and b == -1:
                    pe.wait_ge(w2_rdy, 1)
                rows(y_turn.before(b), [(hT[:, m, :], w2[:, m, :]) for m in range(M1)], bent, tokens_turned)

            def rows_of(u, bank_, tiles, terms, ready=None):
                wait(pe, y_rdy, u - 1)
                for i, j in enumerate(tiles):
                    for n, (lhs, rhs) in enumerate(terms):
                        if ready is not None and i == 0:
                            ready(n)
                        mm = nc.tensor.matmul(ps_y[bank_][:, i * F:(i + 1) * F], lhs[:, j * P:(j + 1) * P], rhs,
                                              start=(n == 0), stop=(n == len(terms) - 1))
                mm.then_inc(y_ps, 1)

            def rows(u, terms, ready=None, after=None):
                for g, tiles in enumerate(GROUPS):
                    rows_of(u + g, g % 2, tiles, terms, ready if g == 0 else None)
                    if after is not None:
                        after(g)

            def turn_rows(src_, j, bank_, u, all_before):
                wait(pe, tr_rdy, u if all_before else u - 1)
                for c in range(KC):
                    mm = nc.tensor.transpose(ps_t[bank_][:, c * P:(c + 1) * P], src_[:, j, c * P:(c + 1) * P],
                                             keep.ident[:, :])
                mm.then_inc(tr_ps, 1)

            def expert_hidden(b, e, after=None):
                u = h_turn.before(b) + CH * (M1 if has_ffn(b) else 0) + e * KC * CH
                i = 0
                for m in range(KC):
                    for c in range(CH):
                        wait(pe, h_rdy, u + i - 3)
                        for k in range(KC):
                            mm = nc.tensor.matmul(ps_h[i % 4][:, 0:CW], ew1[:, e, k, m * P:(m + 1) * P],
                                                  tT[:, k, c * CW:(c + 1) * CW], start=(k == 0), stop=(k == KC - 1))
                        mm.then_inc(h_ps, 1)
                        i += 1
                        if after is not None:
                            after(i - 1)

            def expert_rows(b, e):
                pe.wait_ge(h_rdy, h_turn.before(b) + CH * (M1 if has_ffn(b) else 0) + (e + 1) * KC * CH)
                s = e % 2
                u = y_turn.before(b) + uses(b, e)
                terms = [(hT[:, 2 * s + m, :], ew2[:, e, m, :]) for m in range(KC)]
                for i, (own, g) in enumerate(PLAN[e]):
                    if e == 0 and i == 1:
                        weights_turned(b)
                    if e == 0 and i == 3:
                        pe.wait_ge(tr_rdy, t_turn.before(b) + TB + 3)
                    rows_of(u + i, i % 2, GROUPS[g], terms if own else [(combT[:, :], eb2[:, :])])

            def weights_turned(b):
                pe.wait_ge(lg_rdy, 2 * (b + 1))
                for i, tiles in enumerate((range(0, TB // 2), range(TB // 2, TB))):
                    wait(pe, tr_rdy, t_turn.before(b) + TB + 1 + i)
                    for n, j in enumerate(tiles):
                        mm = nc.tensor.transpose(ps_t[i][0:X, n * P:(n + 1) * P], comb[:, j, :], keep.ident[:, :])
                    mm.then_inc(tr_ps, 1)

            def body(b):
                if has_ffn(b):
                    ffn(b)
                u = t_turn.before(b)
                if has_moe(b):
                    if not has_ffn(b):
                        pe.wait_ge(t_rdy, b + 1)
                        for j in range(TB):
                            turn_rows(t, j, j % 2, u + j, j == 0)
                    pe.wait_ge(tr_rdy, u + TB)

                    def logits(i):
                        per = -(-TB // (KC * CH))
                        for j in range(i * per, min(TB, (i + 1) * per)):
                            for k in range(KC):
                                mm = nc.tensor.matmul(ps_t[1][:, j * X:(j + 1) * X], tT[:, k, j * P:(j + 1) * P],
                                                      router[:, k, :], start=(k == 0), stop=(k == KC - 1))
                            if j == TB - 1:
                                mm.then_inc(tr_ps, 1)
                    expert_hidden(b, 0, logits)
                    for e in range(X):
                        if e + 1 < X:
                            expert_hidden(b, e + 1)
                        expert_rows(b, e)
                        if has_pre(b):
                            for j in spots[e]:
                                if j == 0:
                                    pe.wait_ge(r1_rdy, b + 3)
                                turn_rows(r1, j, j % 2, u + TB + 3 + j, j == 0)
                elif has_pre(b):
                    pe.wait_ge(r1_rdy, b + 3)
                    for j in range(TB):
                        turn_rows(r1, j, j % 2, u + j, j == 0)
                if isinstance(b, int) and b == -1:
                    pe.wait_ge(ew_in, 16 * 2 * X)
            iterations(pe, body)

        @block.scalar
        def _(act):
            act.wait_ge(setup_rdy, 1)

            def r1_evac(b, j, u):
                act.wait_ge(tr_ps, u + 1)
                nc.scalar.activation(r1T[:, :, j * P:(j + 1) * P],
                                     ps_t[j % 2][:, 0:KC * P].rearrange("p (c n) -> p c n", c=KC), ACT.Copy).then_inc(tr_rdy, 1)

            def hidden(b, e):
                u = h_turn.before(b) + CH * (M1 if has_ffn(b) else 0) + e * KC * CH
                s = e % 2
                if e < 2:
                    wait(act, y_ps, y_turn.before(b) + (G if has_ffn(b) else 0))
                else:
                    act.wait_ge(y_ps, y_turn.before(b) + uses(b, e - 1))
                i = 0
                for m in range(KC):
                    for c in range(CH):
                        act.wait_ge(h_ps, u + i + 1)
                        nc.scalar.activation(hT[:, 2 * s + m, c * CW:(c + 1) * CW], ps_h[i % 4][:, 0:CW], ACT.Gelu,
                                             bias=bias[:, 2 * M1 + e * KC + m:2 * M1 + e * KC + m + 1]).then_inc(h_rdy, 1)
                        i += 1

            def body(b):
                if has_ffn(b):
                    u = h_turn.before(b)
                    v = M1 * CH * (b + 1)
                    wait(act, y_ps, y_turn.before(b))
                    i = 0
                    for m in range(M1):
                        for c in range(CH):
                            act.wait_ge(h_ps, u + i + 1)
                            nc.scalar.activation(hT[:, m, c * CW:(c + 1) * CW], ps_h[i % 4][:, 0:CW], ACT.Relu,
                                                 bias=rise_b[:, m:m + 1], scale=rise[:, m:m + 1])
                            wait(act, prelu_rdy, v + i - 1)
                            nc.scalar.activation(bend[:, i % 2, :], ps_h[i % 4][:, 0:CW], ACT.Identity,
                                                 bias=slope_b[:, m:m + 1], scale=slope[:, m:m + 1]).then_inc(h_rdy, 1)
                            i += 1
                u = t_turn.before(b)
                if has_moe(b):
                    hidden(b, 0)
                    act.wait_ge(lg_rdy, 2 * b + 1)
                    nc.scalar.activation(prob[:, :, :], prob[:, :, :], ACT.Exp).then_inc(pe_rdy, 1)
                    for e in range(X):
                        if e + 1 < X:
                            hidden(b, e + 1)
                        if has_pre(b):
                            for j in spots[e]:
                                r1_evac(b, j, u + TB + 3 + j)
                elif has_pre(b):
                    for j in range(TB):
                        r1_evac(b, j, u + j)
            iterations(act, body)

        @block.gpsimd
        def _(pool):
            pool.wait_ge(setup_rdy, 1)

            def body(b):
                if not has_ffn(b):
                    return
                u = h_turn.before(b)
                i = 0
                for m in range(M1):
                    for c in range(CH):
                        h = hT[:, m, c * CW:(c + 1) * CW]
                        pool.wait_ge(h_rdy, u + i + 1)
                        nc.gpsimd.tensor_tensor(h, h, bend[:, i % 2, :], ALU.add).then_inc(prelu_rdy, 1)
                        i += 1
            iterations(pool, body)

        @block.vector
        def _(dve):
            step = Chain(dve, dvec)

            def norm(src_, dst_, affine):
                moments(src_)
                last = centred(src_, dst_)
                if affine:
                    step(last)
                    step(gained(dst_))
                    last = shifted(dst_)
                return last

            def moments(src_):
                for j in range(TB):
                    last = nc.vector.bn_stats(stats[:, j, :], src_[:, j, :])
                step(last, apart=passed)
                for j in range(TB):
                    last = nc.vector.bn_aggr(mv[:, j, :], stats[:, j, :])
                step(last)
                step(nc.vector.tensor_scalar(var[:, :], mv[:, :, 1], EPS, None, ALU.add))
                rsqrt(nc, step, var[:, :], rstd[:, :], tmp[:, :])

            def centred(src_, dst_):
                for j in range(TB):
                    last = nc.vector.tensor_scalar(dst_[:, j, :], src_[:, j, :], mv[:, j, 0:1], rstd[:, j:j + 1],
                                                   ALU.subtract, ALU.mult)
                return last

            def gained(dst_):
                return nc.vector.tensor_tensor(dst_[:, :, :], dst_[:, :, :], over_tiles(ln_g), ALU.mult)

            def shifted(dst_):
                return nc.vector.tensor_tensor(dst_[:, :, :], dst_[:, :, :], over_tiles(ln_b), ALU.add)

            def over_tiles(rows_):
                return rows_[:, :].rearrange("p (a f) -> p a f", a=1).to_broadcast([P, TB, F])

            def pre(b, part):
                c = b + 2
                if part == 0:
                    a = keep.acc[:, bass.ds(c * (TB * FA), TB * FA)].rearrange("p (n c) -> p n c", c=HC)
                    step(nc.vector.tensor_scalar(den[:, :], a[:, :, DH], 1e-30, None, ALU.max))
                    step(nc.vector.reciprocal(den[:, :], den[:, :]))
                    r = r1[:, :, :].rearrange("p t (h d) -> p (t h) d", d=DH)
                    step(nc.vector.tensor_tensor(r, a[:, :, 0:DH], den[:, :].rearrange("p (n a) -> p n a", a=1).to_broadcast(
                        [P, TB * HEADS, DH]), ALU.mult))
                    dve.wait_ge(feat_in, 16 * (c + 1))
                    step(nc.vector.tensor_tensor(r1[:, :, :], r1[:, :, :], feat[:, :, :], ALU.add))
                elif part == 1:
                    moments(r1)
                elif part == 2:
                    step(centred(r1, r1))
                    step(gained(r1))
                else:
                    shifted(r1).then_inc(r1_rdy, 1)

            def pick_best():
                step(nc.vector.tensor_reduce(best[:, 0, :], pick[:, 0, :, :], AX.X, ALU.max))
                step(nc.vector.tensor_tensor(pick[:, 1, :, :], pick[:, 0, :, :], of_tile(best[:, 0, :]), ALU.is_equal))
                step(nc.vector.tensor_tensor(pick[:, 1, :, :], pick[:, 1, :, :], order(), ALU.mult))
                step(nc.vector.tensor_reduce(best[:, 1, :], pick[:, 1, :, :], AX.X, ALU.max))
                step(nc.vector.tensor_tensor(pick[:, 2, :, :], order(), of_tile(best[:, 1, :]), ALU.is_equal))

            def of_tile(v):
                return v.rearrange("p (t a) -> p t a", a=1).to_broadcast([P, TB, X])

            def order():
                return keep.countdown[:, :].rearrange("p (a x) -> p a x", a=1).to_broadcast([P, TB, X])

            def take_tokens(ut, j):
                dve.wait_ge(tr_ps, ut + j + 1)
                nc.vector.tensor_copy(tT[:, :, j * P:(j + 1) * P],
                                      ps_t[j % 2][:, 0:KC * P].rearrange("p (c n) -> p c n", c=KC)).then_inc(tr_rdy, 1)

            def body(b):
                ut, uy = t_turn.before(b), y_turn.before(b)
                if has_moe(b):
                    step(norm(h2, h2, True))
                    dve.wait_ge(x_in, 32 * (b + 1))
                    step(nc.vector.tensor_tensor(xo[:, :, :], xo[:, :, :], h2[:, :, :], ALU.add))
                    step(norm(xo, t, False))
                    dve.sem_inc(t_rdy, 1)
                    step(nc.vector.tensor_tensor(xo[:, :, :], xo[:, :, :], t[:, :, :], ALU.add))
                if has_ffn(b):
                    dve.wait_ge(r1_rdy, b + 2)
                    step(nc.vector.tensor_tensor(h2[:, :, :], r1[:, :, :], over_tiles(b2), ALU.add))
                    if not has_moe(b):
                        dve.wait_ge(tr_rdy, ut)
                        if has_pre(b):
                            for part in range(4):
                                pre(b, part)
                    for g, tiles in enumerate(GROUPS):
                        dve.wait_ge(y_ps, uy + g + 1)
                        n = len(tiles)
                        j = tiles[0]
                        nc.vector.tensor_tensor(h2[:, j:j + n, :], ps_y[g % 2][:, 0:n * F].rearrange("p (n f) -> p n f", n=n),
                                                h2[:, j:j + n, :], ALU.add).then_inc(y_rdy, 1)
                        if has_moe(b):
                            for j in tiles:
                                take_tokens(ut, j)
                    dve.wait_ge(y_rdy, uy + G)
                elif has_moe(b):
                    for j in range(TB):
                        take_tokens(ut, j)
                if has_moe(b):
                    dve.wait_ge(tr_ps, ut + TB + 1)
                    lg = ps_t[1][:, 0:TB * X].rearrange("p (t x) -> p t x", x=X)
                    step(nc.vector.tensor_reduce(best[:, 0, :], lg, AX.X, ALU.max))
                    ins = nc.vector.tensor_tensor(prob[:, :, :], lg, of_tile(best[:, 0, :]), ALU.subtract)
                    ins.then_inc(tr_rdy, 1)
                    dve.wait_ge(tr_rdy, ut + TB + 1)
                    dve.sem_inc(lg_rdy, 1)
                    dve.wait_ge(pe_rdy, b + 1)
                    step(nc.vector.tensor_reduce(best[:, 0, :], prob[:, :, :], AX.X, ALU.add))
                    step(nc.vector.reciprocal(best[:, 0, :], best[:, 0, :]))
                    step(nc.vector.tensor_tensor(prob[:, :, :], prob[:, :, :], of_tile(best[:, 0, :]), ALU.mult))
                    step(nc.vector.tensor_copy(pick[:, 0, :, :], prob[:, :, :]))
                    pick_best()
                    step(nc.vector.scalar_tensor_tensor(out=pick[:, 0, :, :], in0=pick[:, 2, :, :], scalar=-2.0,
                                                        in1=prob[:, :, :], op0=ALU.mult, op1=ALU.add))
                    step(nc.vector.tensor_tensor(comb[:, :, :], pick[:, 2, :, :], prob[:, :, :], ALU.mult))
                    pick_best()
                    step(nc.vector.tensor_tensor(pick[:, 2, :, :], pick[:, 2, :, :], prob[:, :, :], ALU.mult))
                    step(nc.vector.tensor_tensor(comb[:, :, :], comb[:, :, :], pick[:, 2, :, :], ALU.add))
                    step(nc.vector.tensor_reduce(best[:, 0, :], comb[:, :, :], AX.X, ALU.add))
                    step(nc.vector.tensor_scalar(best[:, 0, :], best[:, 0, :], 1e-12, None, ALU.max))
                    step(nc.vector.reciprocal(best[:, 0, :], best[:, 0, :]))
                    nc.vector.tensor_tensor(comb[:, :, :], comb[:, :, :], of_tile(best[:, 0, :]), ALU.mult).then_inc(lg_rdy, 1)
                    dve.wait_ge(lg_rdy, 2 * (b + 1))

                    def weighted(e, bank_, tiles, at):
                        dve.wait_ge(y_ps, at + 1)
                        for i, j in enumerate(tiles):
                            last = nc.vector.scalar_tensor_tensor(
                                out=xo[:, j, :], in0=ps_y[bank_][:, i * F:(i + 1) * F], scalar=comb[:, j, e:e + 1],
                                in1=xo[:, j, :], op0=ALU.mult, op1=ALU.add)
                        last.then_inc(y_rdy, 1)

                    for e in range(X):
                        at = uy + uses(b, e)
                        for i, (own, g) in enumerate(PLAN[e]):
                            tiles = GROUPS[g]
                            if e == 0 and i == 0:
                                for c, some in enumerate((range(0, TB // 2), range(TB // 2, TB))):
                                    dve.wait_ge(tr_ps, ut + TB + 2 + c)
                                    n = len(some) * P
                                    nc.vector.tensor_copy(combT[:, some[0] * P:some[0] * P + n],
                                                          ps_t[c][0:X, 0:n]).then_inc(tr_rdy, 1)
                            if own:
                                if not PLAN[e][i - 1][0]:
                                    dve.wait_ge(y_rdy, at + i)
                                weighted(e, i % 2, tiles, at + i)
                                continue
                            dve.wait_ge(y_ps, at + i + 1)
                            dve.wait_ge(y_rdy, at + i)
                            n, j = len(tiles), tiles[0]
                            nc.vector.tensor_tensor(xo[:, j:j + n, :],
                                                    ps_y[i % 2][:, 0:n * F].rearrange("p (n f) -> p n f", n=n),
                                                    xo[:, j:j + n, :], ALU.add).then_inc(y_rdy, 1)
                        dve.wait_ge(y_rdy, at + len(PLAN[e]))
                        if 1 <= e <= 4 and has_pre(b):
                            pre(b, e - 1)
                    dve.sem_inc(rows_done, 1)
                elif has_pre(b) and not has_ffn(b):
                    for part in range(4):
                        pre(b, part)

            nc.vector.memset(xo[:, :, :], 0.0).then_inc(zero_rdy, 1)
            dve.wait_ge(setup_ps, 1)
            step(nc.vector.tensor_copy(bias[:, :], ps_t[0][:, 0:nrows]))
            step(nc.vector.tensor_scalar(side[:, :], bias[:, M1:2 * M1], 1.0, 2.0, ALU.is_le, ALU.mult))
            step(nc.vector.tensor_scalar(side[:, :], side[:, :], -1.0, None, ALU.add))
            step(nc.vector.tensor_tensor(slope[:, :], side[:, :], bias[:, M1:2 * M1], ALU.mult))
            step(nc.vector.tensor_tensor(rise[:, :], side[:, :], slope[:, :], ALU.subtract))
            step(nc.vector.tensor_tensor(rise_b[:, :], rise[:, :], bias[:, 0:M1], ALU.mult))
            step(nc.vector.tensor_tensor(slope_b[:, :], slope[:, :], bias[:, 0:M1], ALU.mult))
            nc.vector.tensor_copy(router[:, :, :], ps_t[0][:, 64:64 + KC * X].rearrange("p (c x) -> p c x", x=X)).then_inc(setup_rdy, 1)
            dve.wait_ge(small_in, 16 * 8)
            body(-2)
            dve.wait_ge(w2_in, 16)
            for m in range(M1):
                last = nc.vector.tensor_scalar(w2[:, m, :], w2[:, m, :], side[:, m:m + 1], None, ALU.mult)
            last.then_inc(w2_rdy, 1)
            body(-1)
            if NB > 2:
                start = step.k
                with dve.Fori(0, NB - 2) as b:
                    step.base, step.k = b * STEPS + start, 0
                    body(b)
                assert step.k == STEPS, step.k
                step.base, step.k = start + (NB - 2) * STEPS, 0
            body(NB - 2)
            body(NB - 1)


class Keep:
    pass


def build(nc, x, src, dst, Wq, Wk, Wv, ln_g, ln_b, W1, b1, alpha, W2, b2, router, ew1, eb1, ew2, eb2, out, stop=None):
    z = Sizes(x.shape[0], src.shape[0], W1.shape[1], router.shape[0])
    feat_d = nc.dram_tensor("feat_scratch", (z.NT * P, F), F32, kind="ExternalOutput" if stop else "Internal").ap()
    kv_d = nc.dram_tensor("kv_scratch", (z.NT * P, 2 * F), F32, kind="ExternalOutput" if stop else "Internal").ap()
    etab_d = nc.dram_tensor("edge_scratch", (3, z.EP), F32, kind="ExternalOutput" if stop else "Internal").ap()
    pen_d = nc.dram_tensor("pen_scratch", (z.EP + 1,), F32, kind="ExternalOutput" if stop else "Internal").ap()
    with ExitStack() as ctx:
        keep = Keep()

        def sb(name, shape, dt=F32):
            return ctx.enter_context(nc.sbuf_tensor(name, shape, dt))

        keep.acc = sb("acc", [P, z.NT * FA])
        keep.ident = sb("ident", [P, P])
        keep.ones = sb("ones", [P, P])
        keep.iota = sb("iota", [P, P], BF16)
        keep.countdown = sb("countdown", [P, HEADS])
        keep.lastcol = sb("lastcol", [P, 1])
        keep.notlast = sb("notlast", [P, 1])
        with ExitStack() as ctx2:
            def sb2(name, shape, dt=F32):
                return ctx2.enter_context(nc.sbuf_tensor(name, shape, dt))
            keep.q = sb2("q", [P, z.NT * F])
            keep.reset = sb2("reset", [P, z.NI])
            keep.w_i = sb2("w_i", [P, z.NI], I32)
            keep.e_i = sb2("e_i", [P, z.NI], I32)
            keep.minus_first = sb2("minus_first", [P, z.NI])
            node_phase(nc, z, x, src, dst, Wq, Wk, Wv, feat_d, kv_d, etab_d, pen_d, keep)
            edge_phase(nc, z, kv_d, etab_d, pen_d, keep)
        w = Keep()
        w.W1, w.b1, w.alpha, w.W2, w.b2, w.ln_g, w.ln_b = W1, b1, alpha, W2, b2, ln_g, ln_b
        w.router, w.ew1, w.eb1, w.ew2, w.eb2 = router, ew1, eb1, ew2, eb2
        ffn_phase(nc, z, w, x, feat_d, out, keep)
        if stop:
            with ExitStack() as c3:
                s = c3.enter_context(nc.semaphore("dbg"))
                accd = nc.dram_tensor("acc_dbg", (P, z.NT * FA), F32, kind="ExternalOutput").ap()
                blk = c3.enter_context(nc.Block())

                @blk.sync
                def _(sp):
                    sp.dma_start(accd, keep.acc[:, :]).then_inc(s, 16)
                    sp.wait_ge(s, 16)


_INS = ["x", "src", "dst", "L0_gnn_Wq", "L0_gnn_Wk", "L0_gnn_Wv", "L0_gnn_ln_g", "L0_gnn_ln_b", "L0_gnn_W1", "L0_gnn_b1",
        "L0_gnn_prelu_alpha", "L0_gnn_W2", "L0_gnn_b2", "L0_ffn_router_w", "L0_ffn_w1", "L0_ffn_b1", "L0_ffn_w2", "L0_ffn_b2"]
STOP = None


def kernel(**inputs):
    import numpy as _np
    import concourse.bacc as _bacc
    from concourse import mybir as _mybir
    from concourse.bass_utils import run_bass_kernel_spmd as _run

    nc = _bacc.Bacc("TRN2", target_bir_lowering=False, num_devices=1)
    arrays, args = {}, []
    for name in _INS:
        a = _np.ascontiguousarray(inputs[name])
        arrays[f"in_{name}_dram"] = a
        args.append(nc.dram_tensor(f"in_{name}_dram", a.shape, _mybir.dt.from_np(a.dtype), kind="ExternalInput").ap())
    out = nc.dram_tensor("out_0_dram", inputs["x"].shape, F32, kind="ExternalOutput").ap()
    build(nc, *args, out, stop=STOP)
    r = _run(nc, [arrays], core_ids=[0])
    return r.results[0]["out_0_dram"]
```
